# Optimizing a Trainium2 kernel written in Bass

```python
import numpy as np
import jax
import jax.numpy as jnp

def _softmax(x, axis=-1):
    return jax.nn.softmax(x, axis=axis)

def _gelu(x):
    return jax.nn.gelu(x, approximate=True)

def _silu(x):
    return jax.nn.silu(x)

def _sigmoid(x):
    return jax.nn.sigmoid(x)

def _layernorm(x, axis=-1, eps=1e-05):
    m = jnp.mean(x, axis=axis, keepdims=True)
    v = jnp.var(x, axis=axis, keepdims=True)
    return (x - m) / jnp.sqrt(v + eps)

def _scatter_add(tgt, idx, src, axis=0):
    return tgt.at[idx].add(src)

def _segment_sum(src, seg, n):
    return jax.ops.segment_sum(src, seg, n)
kernel_name = 'mk_macaron_d1_jaxref_r8_359144'

def setup_inputs(seed: int=0):
    np.random.seed(seed)
    _w = jnp.asarray

    def _L0_attn_setup():
        import jax, jax.numpy as jnp
        import numpy as np
        N_EMBD = 128
        N_HEAD = 16
        HEAD_SIZE = 64
        LN_EPS = 0.001
        key = jax.random.key(seed)
        ks = jax.random.split(key, 7)
        B, S, D, H, E = (4, 256, N_EMBD, N_HEAD, HEAD_SIZE)
        x = jax.random.normal(ks[0], (B, S, D), dtype=jnp.float32)
        scale = 1.0 / np.sqrt(D)
        Wq = jax.random.normal(ks[1], (H, D, E), dtype=jnp.float32) * scale
        Wk = jax.random.normal(ks[2], (H, D, E), dtype=jnp.float32) * scale
        Wv = jax.random.normal(ks[3], (H, D, E), dtype=jnp.float32) * scale
        Wo = jax.random.normal(ks[4], (H * E, D), dtype=jnp.float32) * scale
        gamma = jnp.ones((D,), dtype=jnp.float32)
        beta = jnp.zeros((D,), dtype=jnp.float32)
        return {'x': x, 'Wq': Wq, 'Wk': Wk, 'Wv': Wv, 'Wo': Wo, 'gamma': gamma, 'beta': beta}
    _L0_attn_in = _L0_attn_setup()

    def _L0_ffn_setup():
        import jax, jax.numpy as jnp
        import numpy as np
        D_MODEL = 128
        D_FF = 512
        N_EXPERTS = 8
        TOP_K = 2

        def _ffn(x, w1, b1, w2, b2):
            h = jax.nn.gelu(x @ w1.T + b1)
            return h @ w2.T + b2
        key = jax.random.key(seed)
        ks = jax.random.split(key, 12)
        s = 0.02
        x = jax.random.normal(ks[0], (4, 256, D_MODEL), dtype=jnp.float32)
        shared_w1 = jax.random.normal(ks[1], (D_FF, D_MODEL), dtype=jnp.float32) * s
        shared_b1 = jnp.zeros((D_FF,), dtype=jnp.float32)
        shared_w2 = jax.random.normal(ks[2], (D_MODEL, D_FF), dtype=jnp.float32) * s
        shared_b2 = jnp.zeros((D_MODEL,), dtype=jnp.float32)
        router_w = jax.random.normal(ks[3], (N_EXPERTS, D_MODEL), dtype=jnp.float32) * s
        router_b = jnp.zeros((N_EXPERTS,), dtype=jnp.float32)
        spec_w1 = jax.random.normal(ks[4], (N_EXPERTS, D_FF, D_MODEL), dtype=jnp.float32) * s
        spec_b1 = jnp.zeros((N_EXPERTS, D_FF), dtype=jnp.float32)
        spec_w2 = jax.random.normal(ks[5], (N_EXPERTS, D_MODEL, D_FF), dtype=jnp.float32) * s
        spec_b2 = jnp.zeros((N_EXPERTS, D_MODEL), dtype=jnp.float32)
        return dict(x=x, shared_w1=shared_w1, shared_b1=shared_b1, shared_w2=shared_w2, shared_b2=shared_b2, router_w=router_w, router_b=router_b, spec_w1=spec_w1, spec_b1=spec_b1, spec_w2=spec_w2, spec_b2=spec_b2)
    _L0_ffn_in = _L0_ffn_setup()
    _d = {'L0_attn_x': _L0_attn_in['x'], 'L0_attn_Wq': _L0_attn_in['Wq'], 'L0_attn_Wk': _L0_attn_in['Wk'], 'L0_attn_Wv': _L0_attn_in['Wv'], 'L0_attn_Wo': _L0_attn_in['Wo'], 'L0_attn_gamma': _L0_attn_in['gamma'], 'L0_attn_beta': _L0_attn_in['beta'], 'L0_ffn_shared_w1': _L0_ffn_in['shared_w1'], 'L0_ffn_shared_b1': _L0_ffn_in['shared_b1'], 'L0_ffn_shared_w2': _L0_ffn_in['shared_w2'], 'L0_ffn_shared_b2': _L0_ffn_in['shared_b2'], 'L0_ffn_router_w': _L0_ffn_in['router_w'], 'L0_ffn_router_b': _L0_ffn_in['router_b'], 'L0_ffn_spec_w1': _L0_ffn_in['spec_w1'], 'L0_ffn_spec_b1': _L0_ffn_in['spec_b1'], 'L0_ffn_spec_w2': _L0_ffn_in['spec_w2'], 'L0_ffn_spec_b2': _L0_ffn_in['spec_b2']}
    _x0 = _d['L0_attn_x']
    _d['L0_attn_x'] = jax.random.normal(jax.random.fold_in(jax.random.key(seed), 1), (2, 1024, 128), dtype=_x0.dtype)
    del _x0
    return _d

def reference(L0_attn_x, L0_attn_Wq, L0_attn_Wk, L0_attn_Wv, L0_attn_Wo, L0_attn_gamma, L0_attn_beta, L0_ffn_shared_w1, L0_ffn_shared_b1, L0_ffn_shared_w2, L0_ffn_shared_b2, L0_ffn_router_w, L0_ffn_router_b, L0_ffn_spec_w1, L0_ffn_spec_b1, L0_ffn_spec_w2, L0_ffn_spec_b2):

    def _L0_attn_ref(x, Wq, Wk, Wv, Wo, gamma, beta):
        import jax, jax.numpy as jnp
        import numpy as np
        N_EMBD = 128
        N_HEAD = 16
        HEAD_SIZE = 64
        LN_EPS = 0.001
        B, S, D = x.shape
        H, _, E = Wq.shape
        q = jnp.einsum('bsd,hde->bhse', x, Wq)
        k = jnp.einsum('bsd,hde->bhse', x, Wk)
        v = jnp.einsum('bsd,hde->bhse', x, Wv)
        scores = jnp.einsum('bhse,bhte->bhst', q, k)
        causal = jnp.tril(jnp.ones((S, S), dtype=bool))
        scores = jnp.where(causal, scores / jnp.sqrt(jnp.float32(E)), jnp.float32(-jnp.inf))
        attn = jax.nn.softmax(scores, axis=-1)
        out = jnp.einsum('bhst,bhte->bhse', attn, v)
        heads = out.transpose(0, 2, 1, 3).reshape(B, S, H * E)
        y = x + heads @ Wo
        mu = jnp.mean(y, axis=-1, keepdims=True)
        var = jnp.mean(jnp.square(y - mu), axis=-1, keepdims=True)
        y = (y - mu) * jax.lax.rsqrt(var + LN_EPS) * gamma + beta
        return y

    def _L0_ffn_ref(x, shared_w1, shared_b1, shared_w2, shared_b2, router_w, router_b, spec_w1, spec_b1, spec_w2, spec_b2):
        import jax, jax.numpy as jnp
        import numpy as np
        D_MODEL = 128
        D_FF = 512
        N_EXPERTS = 8
        TOP_K = 2

        def _ffn(x, w1, b1, w2, b2):
            h = jax.nn.gelu(x @ w1.T + b1)
            return h @ w2.T + b2
        B, T, D = x.shape
        xf = x.reshape(-1, D)
        U = xf.shape[0]
        logits = xf @ router_w.T + router_b
        routing = jax.nn.softmax(logits, axis=-1)
        sel_w, sel_idx = jax.lax.top_k(routing, TOP_K)
        sel_w = sel_w / sel_w.sum(axis=-1, keepdims=True)
        comb = jnp.zeros_like(routing).at[jnp.arange(U)[:, None], sel_idx].set(sel_w)
        shared_out = _ffn(xf, shared_w1, shared_b1, shared_w2, shared_b2)

        def body(acc, params):
            w1, b1, w2, b2, we = params
            return (acc + we[:, None] * _ffn(xf, w1, b1, w2, b2), None)
        acc0 = jnp.zeros_like(shared_out)
        acc, _ = jax.lax.scan(body, acc0, (spec_w1, spec_b1, spec_w2, spec_b2, comb.T))
        return (shared_out + acc).reshape(B, T, D)
    x = L0_attn_x
    x = x + 0.5 * _L0_ffn_ref(_layernorm(x, axis=-1), L0_ffn_shared_w1, L0_ffn_shared_b1, L0_ffn_shared_w2, L0_ffn_shared_b2, L0_ffn_router_w, L0_ffn_router_b, L0_ffn_spec_w1, L0_ffn_spec_b1, L0_ffn_spec_w2, L0_ffn_spec_b2)
    x = x + _L0_attn_ref(_layernorm(x, axis=-1), L0_attn_Wq, L0_attn_Wk, L0_attn_Wv, L0_attn_Wo, L0_attn_gamma, L0_attn_beta)
    x = x + 0.5 * _L0_ffn_ref(_layernorm(x, axis=-1), L0_ffn_shared_w1, L0_ffn_shared_b1, L0_ffn_shared_w2, L0_ffn_shared_b2, L0_ffn_router_w, L0_ffn_router_b, L0_ffn_spec_w1, L0_ffn_spec_b1, L0_ffn_spec_w2, L0_ffn_spec_b2)
    return x

_drawn_inputs = setup_inputs


def setup_inputs(seed=0):
    import zlib

    import numpy as np

    out = dict(_drawn_inputs(seed))
    spreads = {'L0_attn_gamma': (1.0, 0.2),
     'L0_attn_beta': (0.0, 0.1),
     'L0_ffn_shared_b1': (0.0, 0.334),
     'L0_ffn_shared_b2': (0.0, 0.1),
     'L0_ffn_router_b': (0.0, 0.1),
     'L0_ffn_spec_b1': (0.0, 0.516),
     'L0_ffn_spec_b2': (0.0, 0.1)}
    factors = {}
    for name, (base, spread) in spreads.items():
        noise = np.random.default_rng([zlib.crc32(name.encode()), seed]).standard_normal(out[name].shape)
        drawn = base * np.exp(spread * noise) if base else spread * noise
        out[name] = jnp.asarray(drawn.astype(out[name].dtype))
    for name, factor in factors.items():
        out[name] = (out[name] * factor).astype(out[name].dtype)
    return out
```

```python
import concourse.bass as bass
from concourse import mybir
from contextlib import ExitStack, contextmanager


def macaron_block_kernel(nc, x, w1s, w1e, w2s, w2e, b1s, b1e, b2s, b2e, rw, rb, wq, wk, wv, wo, gamma, beta, out):
    f32, f16, bf16 = mybir.dt.float32, mybir.dt.float16, mybir.dt.bfloat16
    ALU, ACT, AX = mybir.AluOpType, mybir.ActivationFunctionType, mybir.AxisListType

    P = 128
    D = x.shape[2]
    NT = x.shape[1]
    S = 1024
    NB = NT * P // S
    QT = S // P
    E = wq.shape[2]
    NH = wq.shape[1]
    NEX = w1e.shape[1] + 1
    F = w1e.shape[2]
    FC = F // P
    TB = 4
    NBLK = NT // TB
    BLK = TB * P
    EPS, EPS_Y = 1e-5, 1e-3
    W1_UP = 64.0
    WA_UP = 16.0
    M_UP = 64.0
    NEG = -1e30
    SCALE = float(E) ** -0.5
    NHEADS = NB * NH
    VW = E + 1
    PAIRS = NH * E // P

    KCH = [(j, P * j, 512 - P * j) for j in range(4)] + [(j, 512, 512) for j in range(4)] + \
          [(j, P * j, S - P * j) for j in range(4, QT)]
    NCH = len(KCH)
    POFF = [sum(c[2] for c in KCH[:k]) for k in range(NCH)]
    PW = sum(c[2] for c in KCH)
    KIDX = {(j, 0 if q0 < 512 else 1): k for k, (j, q0, n) in enumerate(KCH)}
    DIAG = [k for k, (j, q0, n) in enumerate(KCH) if q0 == P * j]
    by_width = {}
    for ch in [(i, 0, P * (i + 1)) for i in range(4)] + \
            [c for i in range(4, QT) for c in ((i, 0, 512), (i, 512, P * (i + 1) - 512))]:
        by_width.setdefault(ch[2], []).append(ch)
    QCH = [by_width[n].pop() for n in (512, 512, 384, 256, 512, 512, 128, 256, 512, 384, 512, 128)]
    assert len(QCH) == NCH and not any(by_width.values())
    BLOCKS = [(i, j) for i in range(QT) for j in range(i + 1)]
    BPS = len(BLOCKS) // NCH
    POOL_LO = [4, 6]
    MT_SLOT = 6
    PROJ_SLOTS = {0: 0, 3: 1}
    T_SLOTS = {1: 0, 3: 1}
    WO_SLOTS = {5: 0, 7: 1}
    V_SLOT = 10

    nc.disable_value_cache = True

    @contextmanager
    def kept_addresses():
        nc.disable_value_cache = False
        yield
        nc.disable_value_cache = True

    ctx = ExitStack()
    with ctx:
        def sb(name, shape, dt=f32):
            return ctx.enter_context(nc.sbuf_tensor(name, shape, dt))

        def sem(name):
            return ctx.enter_context(nc.semaphore(name))

        bank = [ctx.enter_context(nc.psum_tensor(f"bank{i}", [P, 512], f32)) for i in range(8)]

        res = sb("res", [P, NT, D])
        acc = sb("acc", [P, NT, D])
        xn = sb("xn", [P, NT, D])
        xh = sb("xh", [P, NT * P], f16)
        xl = sb("xl", [P, NT * P], f16)
        stats = sb("stats", [P, NT, 6])
        mv = sb("mv", [P, NT, 2])
        veps = sb("veps", [P, NT])
        sd = sb("sd", [P, NT])
        rstd = sb("rstd", [P, NT])
        w1h = sb("w1h", [P, NEX * F], f16)
        w1l = sb("w1l", [P, NEX * F], f16)
        w2 = sb("w2", [P, NEX, FC, D])
        b1 = sb("b1", [P, NEX * FC])
        b2 = sb("b2", [NEX, D])
        rw_sb = sb("rw_sb", [P, NEX - 1])
        rb_sb = sb("rb_sb", [P, NEX - 1])
        wqk_h = sb("wqk_h", [P, NH * 2 * E], f16)
        wqk_l = sb("wqk_l", [P, NH * 2 * E], f16)
        wqk_h4, wqk_l4 = (w[:, :].rearrange("p (h i e) -> p h i e", i=2, h=NH) for w in (wqk_h, wqk_l))
        wv_h = sb("wv_h", [P, NH * E], f16)
        wv_l = sb("wv_l", [P, NH * E], f16)
        wo_sb = sb("wo_sb", [P, PAIRS, D])
        gam = sb("gam", [P, D])
        bet = sb("bet", [P, D])
        identf = sb("identf", [P, P])
        identh = sb("identh", [P, P], f16)
        identb = sb("identb", [P, P], bf16)
        tri = sb("tri", [P, P], bf16)
        rev = sb("rev", [P, NEX - 1])
        lg = sb("lg", [P, NT, NEX - 1])
        lg2 = sb("lg2", [P, NT, NEX - 1])
        pr = sb("pr", [P, NT, NEX - 1])
        rk = sb("rk", [P, NT, NEX - 1])
        sel = [sb(f"sel{i}", [P, NT, NEX - 1]) for i in range(2)]
        top = [sb(f"top{i}", [P, NT]) for i in range(2)]
        first = sb("first", [P, NT])
        comb = sb("comb", [P, NT, NEX])
        probs = [sb(f"probs{i}", [P, 2 * PW], f16) for i in range(2)]
        ph = [t[:, 0:PW] for t in probs]
        pl = [t[:, PW:2 * PW] for t in probs]
        NRING = 6
        p32 = [sb(f"p32_{i}", [P, 512]) for i in range(NRING)]
        hh = [sb(f"hh{i}", [P, S], f16) for i in range(2)]
        ll = [sb(f"ll{i}", [P, S], f16) for i in range(2)]
        qsks = sb("qsks", [P, 8 * S], f16)
        qs = [qsks[:, i * S:(i + 1) * S] for i in range(4)]
        ks = [qsks[:, (4 + i) * S:(5 + i) * S] for i in range(4)]
        qms = sb("qms", [E + 2, 4 * S], f16)
        qm = [qms[:, i * S:(i + 1) * S] for i in range(4)]
        km = [sb(f"km{i}", [E + 2, S], f16) for i in range(4)]
        vh = [sb(f"vh{i}", [P, QT, VW], f16) for i in range(4)]
        vl = [sb(f"vl{i}", [P, QT, E], f16) for i in range(4)]
        v32 = [sb(f"v32_{i}", [P, QT, E]) for i in range(2)]
        hpair = [sb(f"hpair{i}", [P, QT, 2 * E]) for i in range(NB)]
        hpT = [sb(f"hpT{i}", [P, BLK]) for i in range(2)]
        stage = probs[0][:, :].bitcast(f32)[:, 0:NEX * F]
        xT = probs[1][:, :].bitcast(f32)[:, 0:NT * P]
        hid = [qsks[:, :].bitcast(f32)[:, i * FC * BLK:(i + 1) * FC * BLK].rearrange("p (c n) -> p c n", c=FC)
               for i in range(2)]
        combT = qms[:, :].bitcast(f32)[0:NEX, :]
        mpart = sb("mpart", [P, QT, 2])
        negm = sb("negm", [P, QT])
        mhl = sb("mhl", [P, 2 * QT], f16)
        mrows = sb("mrows", [2 * QT, P], f16)
        rsum = sb("rsum", [P, 2, TB])

        S_BANK, A_BANK, O_BANK, J_BANK, V_BANK = bank[0:2], bank[2:4], bank[4:6], bank[6], bank[7]
        H_BANK, Y_BANK, R_BANK, T_BANK = bank[0:4], bank[4:6], bank[6], bank[6:8]

        x_in, rw_in, w1_in, w2_in, b_in, wa_in, wo_in = (sem(n) for n in
            ("x_in", "rw_in", "w1_in", "w2_in", "b_in", "wa_in", "wo_in"))
        w1s_in, out_done = sem("w1s_in"), sem("out_done")
        const_ready, whi_ready, wlo_ready = sem("const_ready"), sem("whi_ready"), sem("wlo_ready")
        zeroed = sem("zeroed")
        var_ready, sd_ready, xn_ready = sem("var_ready"), sem("sd_ready"), sem("xn_ready")
        xT_psum, xT_ready, xh_ready, xl_ready = sem("xT_psum"), sem("xT_ready"), sem("xh_ready"), sem("xl_ready")
        lg_psum, lgm_ready, pr_ready, comb_ready = sem("lg_psum"), sem("lgm_ready"), sem("pr_ready"), sem("comb_ready")
        h_psum, hid_ready, y_psum, acc_ready = sem("h_psum"), sem("hid_ready"), sem("y_psum"), sem("acc_ready")
        cT_psum, cT_ready, b2_psum, b2_added, res_ready = (sem(n) for n in
            ("cT_psum", "cT_ready", "b2_psum", "b2_added", "res_ready"))
        v_psum, v_ready = sem("v_psum"), sem("v_ready")
        proj_done, hi_ready, lo_ready, stack_in = sem("proj_done"), sem("hi_ready"), sem("lo_ready"), sem("stack_in")
        ph_ready, pl_ready, pool_lo_ready = sem("ph_ready"), sem("pl_ready"), sem("pool_lo_ready")
        v32_ready, vl_ready = sem("v32_ready"), sem("vl_ready")
        aux_done, max_done, mhl_ready, mT_psum, mrows_ready, mrow_in = (sem(n) for n in
            ("aux_done", "max_done", "mhl_ready", "mT_psum", "mrows_ready", "mrow_in"))
        main_done, exp_done, mask_done, pv_done, norm_done = (sem(n) for n in
            ("main_done", "exp_done", "mask_done", "pv_done", "norm_done"))
        hT_psum, hT_ready, wo_psum, y_ready = sem("hT_psum"), sem("hT_ready"), sem("wo_psum"), sem("y_ready")
        dve_step, pool_step = sem("dve_step"), sem("pool_step")

        def head_of(it, c):
            return it * 2 + c // 2 if it is not None else c // 2

        def cnt(per, it, c, plus=0):
            return per * c + plus if it is None else it * (4 * per) + (per * c + plus)

        def wait_count(eng, s, v):
            if not isinstance(v, int) or v > 0:
                eng.wait_ge(s, v)

        def pair_cnt(per, it, c, plus=0):
            done = 2 * (c // 4) + (c % 2)
            return per * done + plus if it is None else it * (2 * per) + (per * done + plus)

        def wait_split(eng, it, c, k):
            while k < 0:
                c, k = c - 1, k + NCH
            if k in POOL_LO:
                wait_count(eng, pool_lo_ready, cnt(len(POOL_LO), it, c, POOL_LO.index(k) + 1))
            else:
                before = len([j for j in range(k) if j not in POOL_LO])
                wait_count(eng, pl_ready, cnt(NCH - len(POOL_LO), it, c, before + 1))

        def ends_pair(n, it, c):
            return live(n, it, c) and n % 4 >= 2

        def live(n, it, c):
            return it is not None or 0 <= n < NHEADS

        FIRST = 2
        LAST = FIRST + (NHEADS - 3 - FIRST) // 4 * 4 - 1

        def run_periods(eng, period):
            for t in range(-3, FIRST):
                period(None, t)
            with eng.Fori(0, (LAST + 1 - FIRST) // 4) as it:
                for c in range(FIRST, FIRST + 4):
                    period(it, c)
            for t in range(LAST + 1, NHEADS + 2):
                period(None, t)

        block = ctx.enter_context(nc.Block())

        @block.sync
        def _(sp):
            sp.dma_start(res[:, :, :], x).then_inc(x_in, 16)
            sp.dma_start(rw_sb[:, :], rw).then_inc(rw_in, 16)
            sp.dma_start(rb_sb[:, :], rb.partition_broadcast(P)).then_inc(rw_in, 16)
            sp.dma_start(stage[:, 0:F], w1s).then_inc(w1s_in, 16)
            sp.dma_start(stage[:, F:], w1e.rearrange("p e f -> p (e f)")).then_inc(w1_in, 16)
            sp.dma_start(b1[:, 0:FC], b1s).then_inc(b_in, 16)
            sp.dma_start(b1[:, FC:], b1e.rearrange("p e f -> p (e f)")).then_inc(b_in, 16)
            sp.dma_start(b2[0:1, :], b2s).then_inc(b_in, 16)
            sp.dma_start(b2[1:NEX, :], b2e).then_inc(b_in, 16)
            sp.dma_start(w2[:, 0], w2s).then_inc(w2_in, 16)
            sp.dma_start(w2[:, 1:], w2e).then_inc(w2_in, 16)
            sp.dma_start(gam[:, :], gamma.partition_broadcast(P)).then_inc(wo_in, 16)
            sp.dma_start(bet[:, :], beta.partition_broadcast(P)).then_inc(wo_in, 16)
            sp.dma_start(wo_sb[:, :, :], wo).then_inc(wo_in, 16)
            sp.wait_ge(whi_ready, NEX)
            sp.wait_ge(wlo_ready, NEX)
            for i, w in enumerate((wq, wk, wv)):
                sp.dma_start(stage[:, i * NH * E:(i + 1) * NH * E], w.rearrange("p h e -> p (h e)")).then_inc(wa_in, 16)

            def period(it, c):
                if live(c + 3, it, c):
                    b, r = (c + 3) % 4, (c + 3) % 2
                    wait_count(sp, main_done, cnt(NCH, it, c, 0))
                    wait_count(sp, stack_in, cnt(16 * 6, it, c, 3 * 16 * 6))
                    sp.wait_ge(hi_ready, cnt(2, it, c, 8))
                    sp.dma_start(qs[b][0:E, :], hh[r][0:E, :]).then_inc(stack_in, 16)
                    sp.dma_start(qm[b][0:E, :], hh[r][0:E, :]).then_inc(stack_in, 16)
                    sp.dma_start(ks[b][0:E, :], hh[r][E:P, :]).then_inc(stack_in, 16)
                    sp.dma_start(ks[b][E:P, :], hh[r][E:P, :]).then_inc(stack_in, 16)
                    sp.wait_ge(lo_ready, cnt(2, it, c, 8))
                    sp.dma_start(qs[b][E:P, :], ll[r][0:E, :]).then_inc(stack_in, 16)
                    sp.dma_start(km[b][0:E, :], ll[r][E:P, :]).then_inc(stack_in, 16)
                if live(c + 1, it, c):
                    sp.wait_ge(mrows_ready, cnt(1, it, c, 2))
                    sp.dma_start(qm[(c + 1) % 4][E:E + 2, :].rearrange("r (i q) -> r i q", i=QT),
                                 mrows[:, :]).then_inc(mrow_in, 16)
            run_periods(sp, period)
            for g in range(NBLK):
                sp.wait_ge(res_ready, 2 * NBLK + g + 1)
                sp.dma_start(out[:, TB * g:TB * (g + 1), :], res[:, TB * g:TB * (g + 1), :]).then_inc(out_done, 16)
            sp.wait_ge(out_done, 16 * NBLK)

        @block.gpsimd
        def _(pool):
            steps = [0]

            def link(ins):
                steps[0] += 1
                ins.then_inc(pool_step, 1)
                pool.wait_ge(pool_step, steps[0])

            for t in (identf, identh, identb):
                link(nc.gpsimd.memset(t[:, :], 0.0))
                link(nc.gpsimd.affine_select(out=t[:, :], in_=t[:, :], compare_op=ALU.not_equal, fill=1.0, base=0,
                                             pattern=[[-1, P]], channel_multiplier=1))
            link(nc.gpsimd.memset(tri[:, :], 0.0))
            link(nc.gpsimd.affine_select(out=tri[:, :], in_=tri[:, :], compare_op=ALU.is_ge, fill=NEG, base=0,
                                         pattern=[[-1, P]], channel_multiplier=1))
            for e in range(NEX - 1):
                link(nc.gpsimd.memset(rev[:, e:e + 1], float(NEX - 1 - e)))
            for i in range(4):
                link(nc.gpsimd.memset(km[i][E:E + 2, :], M_UP))
            nc.gpsimd.memset(mpart[:, :, :], -3e38)
            nc.gpsimd.memset(comb[:, :, 0:1], 1.0)
            for i in range(4):
                nc.gpsimd.memset(vh[i][:, :, E:VW], 1.0)
            nc.gpsimd.memset(acc[:, :, :], 0.0).then_inc(const_ready, 1)

            def period(it, c):
                if live(c, it, c):
                    for k in sorted(DIAG + POOL_LO):
                        if k in POOL_LO:
                            n = KCH[k][2]
                            pool.wait_ge(ph_ready, cnt(NCH, it, c, k + 1))
                            nc.gpsimd.tensor_tensor(pl[c % 2][:, POFF[k]:POFF[k] + n], p32[k % NRING][:, 0:n],
                                                    ph[c % 2][:, POFF[k]:POFF[k] + n],
                                                    ALU.subtract).then_inc(pool_lo_ready, 1)
                            continue
                        pool.wait_ge(exp_done, cnt(NCH, it, c, k + 1))
                        pool.nop(nofuse=True)
                        d = p32[k % NRING][:, 0:P]
                        nc.gpsimd.affine_select(out=d, in_=d, compare_op=ALU.is_ge, fill=0.0, base=0,
                                                pattern=[[1, P]], channel_multiplier=-1).then_inc(mask_done, 1)
                if live(c + 1, it, c):
                    pool.wait_ge(v32_ready, cnt(1, it, c, 2))
                    nc.gpsimd.tensor_tensor(vl[(c + 1) % 4][:, :, :], v32[(c + 1) % 2][:, :, :],
                                            vh[(c + 1) % 4][:, :, 0:E], ALU.subtract).then_inc(vl_ready, 1)
            run_periods(pool, period)
            pool.wait_ge(xn_ready, 3 * NT)
            nc.gpsimd.memset(acc[:, :, :], 0.0).then_inc(zeroed, 1)

        @block.scalar
        def _(act):
            def root(u):
                act.wait_ge(var_ready, u + 1)
                nc.scalar.activation(sd[:, :], veps[:, :], ACT.Sqrt).then_inc(sd_ready, 1)

            def evacuate_transposes(v):
                for g in range(NBLK):
                    act.wait_ge(xT_psum, v * NBLK + g + 1)
                    nc.scalar.copy(xT[:, g * BLK:(g + 1) * BLK], T_BANK[g % 2][:, :]).then_inc(xT_ready, 1)
                    nc.scalar.copy(xh[:, g * BLK:(g + 1) * BLK], T_BANK[g % 2][:, :]).then_inc(xh_ready, 1)

            def ffn(f):
                act.wait_ge(lgm_ready, f + 1)
                nc.scalar.activation(pr[:, :, :], pr[:, :, :], ACT.Exp).then_inc(pr_ready, 1)

                def gelu_step(it, c):
                    e = c // NBLK if it is None else it + c // NBLK
                    for j in range(FC):
                        act.wait_ge(h_psum, cnt(FC, it, c, f * NEX * NBLK * FC + j + 1))
                        wait_count(act, y_psum, cnt(TB, it, c, TB * (f * NEX * NBLK - 1)))
                        act.nop(nofuse=True)
                        nc.scalar.activation(hid[c % 2][:, j, :], H_BANK[j][:, :], ACT.Gelu_apprx_tanh,
                                             bias=b1[:, bass.ds(e * FC + j, 1)],
                                             scale=1.0 / W1_UP).then_inc(hid_ready, 1)
                if f == 0:
                    act.wait_ge(b_in, 64)
                for s in range(3):
                    gelu_step(None, s)
                with act.Fori(0, NEX - 1) as it:
                    for c in range(3, 3 + NBLK):
                        gelu_step(it, c)
                for s in range(NBLK * (NEX - 1) + 3, NBLK * NEX):
                    gelu_step(None, s)
                for g in range(NBLK):
                    act.wait_ge(cT_psum, f * NBLK + g + 1)
                    nc.scalar.copy(combT[:, g * BLK:(g + 1) * BLK], T_BANK[g % 2][0:NEX, :]).then_inc(cT_ready, 1)

            for e in range(NEX):
                act.wait_ge(w1s_in if e == 0 else w1_in, 16)
                nc.scalar.mul(w1h[:, e * F:(e + 1) * F], stage[:, e * F:(e + 1) * F], W1_UP).then_inc(whi_ready, 1)
                if e == 0:
                    root(0)
                    evacuate_transposes(0)
            act.wait_ge(wa_in, 48)
            for i in range(2):
                src = stage[:, i * NH * E:(i + 1) * NH * E].rearrange("p (h e) -> p h e", e=E)
                nc.scalar.mul(wqk_h4[:, :, i, :], src, WA_UP).then_inc(whi_ready, 1)
            nc.scalar.mul(wv_h[:, :], stage[:, 2 * NH * E:3 * NH * E], WA_UP).then_inc(whi_ready, 1)

            ffn(0)
            root(1)
            evacuate_transposes(1)
            def period(it, c):
                for k in range(NCH):
                    if live(c, it, c):
                        j, q0, n = KCH[k]
                        act.wait_ge(main_done, cnt(NCH, it, c, k + 1))
                        wait_split(act, it, c, k - NRING)
                        nc.scalar.activation(p32[k % NRING][:, 0:n], S_BANK[k % 2][:, 0:n], ACT.Exp,
                                             scale=SCALE).then_inc(exp_done, 1)
                    k1, c1 = (k - 1) % NCH, c if k >= 1 else c - 1
                    if live(c1, it, c):
                        n = KCH[k1][2]
                        if k1 in DIAG:
                            act.wait_ge(mask_done, cnt(8, it, c1, DIAG.index(k1) + 1))
                        else:
                            act.wait_ge(exp_done, cnt(NCH, it, c1, k1 + 1))
                        if k1 == 0:
                            wait_count(act, pv_done, cnt(2, it, c, -2))
                        nc.scalar.copy(ph[c1 % 2][:, POFF[k1]:POFF[k1] + n], p32[k1 % NRING][:, 0:n]).then_inc(ph_ready, 1)
                    if k == MT_SLOT + 1 and live(c + 1, it, c):
                        act.wait_ge(mT_psum, cnt(1, it, c, 2))
                        wait_count(act, mrow_in, cnt(16, it, c, 16))
                        nc.scalar.copy(mrows[:, :], J_BANK[:, :].bitcast(f16)[0:2 * QT, 0:P]).then_inc(mrows_ready, 1)
                    if k - 1 in PROJ_SLOTS and live(c + 3, it, c):
                        g = PROJ_SLOTS[k - 1]
                        act.wait_ge(proj_done, cnt(2, it, c, 6 + g + 1))
                        if g == 0:
                            wait_count(act, stack_in, cnt(16 * 6, it, c, 2 * 16 * 6))
                        nc.scalar.mul(hh[(c + 3) % 2][:, 512 * g:512 * g + 512], J_BANK[:, :],
                                      1.0 / WA_UP).then_inc(hi_ready, 1)
                    if k in T_SLOTS and ends_pair(c - 2, it, c):
                        q = T_SLOTS[k]
                        act.wait_ge(hT_psum, pair_cnt(2, it, c - 2, q + 1))
                        nc.scalar.copy(hpT[q][:, :], V_BANK[:, :]).then_inc(hT_ready, 1)
                    if k == V_SLOT and live(c + 1, it, c):
                        act.wait_ge(v_psum, cnt(1, it, c, 2))
                        nc.scalar.mul(vh[(c + 1) % 4][:, :, 0:E], V_BANK[:, :].rearrange("p (t e) -> p t e", e=E),
                                      1.0 / WA_UP).then_inc(v_ready, 1)
                        wait_count(act, vl_ready, cnt(1, it, c, 0))
                        nc.scalar.mul(v32[(c + 1) % 2][:, :, :], V_BANK[:, :].rearrange("p (t e) -> p t e", e=E),
                                      1.0 / WA_UP).then_inc(v32_ready, 1)
            run_periods(act, period)
            root(2)
            root(3)
            evacuate_transposes(2)
            ffn(1)

        @block.vector
        def _(dve):
            steps = [0]

            def link(ins):
                steps[0] += 1
                ins.then_inc(dve_step, 1)
                dve.wait_ge(dve_step, steps[0])

            def norm(u, src, eps):
                for t in range(NT):
                    last = nc.vector.bn_stats(stats[:, t, :], src[:, t, :])
                link(last)
                for t in range(NT):
                    last = nc.vector.bn_aggr(mv[:, t, :], stats[:, t, :])
                link(last)
                nc.vector.tensor_scalar(veps[:, :], mv[:, :, 1], eps, None, ALU.add).then_inc(var_ready, 1)
                dve.wait_ge(sd_ready, u + 1)
                link(nc.vector.reciprocal(rstd[:, :], sd[:, :]))
                for t in range(NT):
                    nc.vector.tensor_scalar(xn[:, t, :], src[:, t, :], mv[:, t, 0:1], rstd[:, t:t + 1],
                                            ALU.subtract, ALU.mult).then_inc(xn_ready, 1)

            def low_parts(v):
                for g in range(NBLK):
                    dve.wait_ge(xh_ready, v * NBLK + g + 1)
                    cols = slice(g * BLK, (g + 1) * BLK)
                    nc.vector.tensor_tensor(xl[:, cols], xT[:, cols], xh[:, cols], ALU.subtract).then_inc(xl_ready, 1)

            def over(t):
                return t[:, :].unsqueeze(2).to_broadcast([P, NT, NEX - 1])

            def pick(i, src):
                link(nc.vector.tensor_reduce(top[i][:, :], src, AX.X, ALU.max))
                link(nc.vector.tensor_tensor(rk[:, :, :], src, over(top[i]), ALU.is_equal))
                rv = rev[:, :].unsqueeze(1).to_broadcast([P, NT, NEX - 1])
                link(nc.vector.tensor_tensor(rk[:, :, :], rk[:, :, :], rv, ALU.mult))
                link(nc.vector.tensor_reduce(first[:, :], rk[:, :, :], AX.X, ALU.max))
                link(nc.vector.tensor_tensor(sel[i][:, :, :], rk[:, :, :], over(first), ALU.is_equal))

            def router(f):
                dve.wait_ge(lg_psum, f + 1)
                rbv = rb_sb[:, :].unsqueeze(1).to_broadcast([P, NT, NEX - 1])
                link(nc.vector.tensor_tensor(lg[:, :, :], R_BANK[:, 0:NT * (NEX - 1)].rearrange("p (t e) -> p t e", t=NT),
                                             rbv, ALU.add))
                pick(0, lg[:, :, :])
                nc.vector.tensor_tensor(pr[:, :, :], lg[:, :, :], over(top[0]), ALU.subtract).then_inc(lgm_ready, 1)
                link(nc.vector.scalar_tensor_tensor(lg2[:, :, :].rearrange("p t e -> p (t e)"),
                                                    sel[0][:, :, :].rearrange("p t e -> p (t e)"), NEG,
                                                    lg[:, :, :].rearrange("p t e -> p (t e)"), ALU.mult, ALU.add))
                pick(1, lg2[:, :, :])
                link(nc.vector.tensor_tensor(sel[0][:, :, :], sel[0][:, :, :], sel[1][:, :, :], ALU.add))
                dve.wait_ge(pr_ready, f + 1)
                link(nc.vector.tensor_tensor(lg2[:, :, :], pr[:, :, :], sel[0][:, :, :], ALU.mult))
                link(nc.vector.tensor_reduce(first[:, :], lg2[:, :, :], AX.X, ALU.add))
                link(nc.vector.reciprocal(top[1][:, :], first[:, :]))
                nc.vector.tensor_tensor(comb[:, :, 1:NEX], lg2[:, :, :], over(top[1]), ALU.mult).then_inc(comb_ready, 1)

            def ffn(f):
                router(f)
                dve.wait_ge(comb_ready, f + 1)
                base = f * NEX * NBLK

                def combine_step(it, c):
                    e = c // NBLK if it is None else it + c // NBLK
                    for j in range(TB):
                        t = TB * (c % NBLK) + j
                        if j == 0:
                            dve.wait_ge(y_psum, cnt(TB, it, c, TB * (base + 1)))
                        if c >= NBLK:
                            dve.wait_ge(acc_ready, cnt(TB, it, c, TB * base + j + 1 - TB * NBLK))
                        nc.vector.scalar_tensor_tensor(acc[:, t, :], Y_BANK[c % 2][:, j * P:(j + 1) * P],
                                                       comb[:, t, bass.ds(e, 1)], acc[:, t, :],
                                                       ALU.mult, ALU.add).then_inc(acc_ready, 1)
                if f == 1:
                    dve.wait_ge(zeroed, 1)
                for s in range(NBLK):
                    combine_step(None, s)
                with dve.Fori(0, NEX - 1) as it:
                    for c in range(NBLK, 2 * NBLK):
                        combine_step(it, c)
                dve.wait_ge(acc_ready, TB * (base + NEX * NBLK))
                for g in range(NBLK):
                    dve.wait_ge(b2_psum, f * NBLK + g + 1)
                    av = acc[:, TB * g:TB * (g + 1), :].rearrange("p t d -> p (t d)")
                    rv = res[:, TB * g:TB * (g + 1), :].rearrange("p t d -> p (t d)")
                    ins = nc.vector.tensor_tensor(av, H_BANK[g][:, :], av, ALU.add)
                    ins.then_inc(b2_added, 1)
                    dve.wait_ge(b2_added, f * NBLK + g + 1)
                    ins = nc.vector.scalar_tensor_tensor(rv, av, 0.5, rv, ALU.mult, ALU.add)
                    ins.then_inc(res_ready, 1)
                dve.wait_ge(res_ready, (2 * f + 1) * NBLK)

            dve.wait_ge(const_ready, 1)
            dve.wait_ge(x_in, 16)
            norm(0, res, EPS)
            def split_w1(e):
                dve.wait_ge(whi_ready, e + 1)
                cols = slice(e * F, (e + 1) * F)
                nc.vector.scalar_tensor_tensor(w1l[:, cols], stage[:, cols], W1_UP, w1h[:, cols],
                                               ALU.mult, ALU.subtract).then_inc(wlo_ready, 1)
            split_w1(0)
            low_parts(0)
            dve.wait_ge(rw_in, 32)
            for e in range(1, NEX):
                split_w1(e)
            for i in range(2):
                dve.wait_ge(whi_ready, NEX + i + 1)
                src = stage[:, i * NH * E:(i + 1) * NH * E].rearrange("p (h e) -> p h e", e=E)
                nc.vector.scalar_tensor_tensor(wqk_l4[:, :, i, :], src, WA_UP, wqk_h4[:, :, i, :],
                                               ALU.mult, ALU.subtract).then_inc(wlo_ready, 1)
            dve.wait_ge(whi_ready, NEX + 3)
            nc.vector.scalar_tensor_tensor(wv_l[:, :], stage[:, 2 * NH * E:3 * NH * E], WA_UP, wv_h[:, :],
                                           ALU.mult, ALU.subtract).then_inc(wlo_ready, 1)
            ffn(0)
            norm(1, res, EPS)
            low_parts(1)
            dve.wait_ge(xn_ready, 2 * NT)
            nc.vector.tensor_copy(acc[:, :, :], xn[:, :, :]).then_inc(y_ready, 1)

            def period(it, c):
                for k in range(NCH):
                    if live(c + 2, it, c):
                        i, k0, n = QCH[k]
                        dve.wait_ge(aux_done, cnt(NCH, it, c, 2 * NCH + k + 1))
                        if k == 0:
                            wait_count(dve, mhl_ready, cnt(3, it, c, 4))
                        nc.vector.tensor_reduce(mpart[:, i, k0 // 512:k0 // 512 + 1], A_BANK[k % 2][:, 0:n], AX.X,
                                                ALU.max).then_inc(max_done, 1)
                    if k - 1 in PROJ_SLOTS and live(c + 3, it, c):
                        g, r = PROJ_SLOTS[k - 1], (c + 3) % 2
                        cols = slice(512 * g, 512 * g + 512)
                        dve.wait_ge(hi_ready, cnt(2, it, c, 6 + g + 1))
                        if g == 0:
                            wait_count(dve, stack_in, cnt(16 * 6, it, c, 2 * 16 * 6))
                        nc.vector.scalar_tensor_tensor(ll[r][:, cols], J_BANK[:, :], 1.0 / WA_UP, hh[r][:, cols],
                                                       ALU.mult, ALU.subtract).then_inc(lo_ready, 1)
                    k2, c2 = (k - 2) % NCH, c if k >= 2 else c - 1
                    if live(c2, it, c) and k2 not in POOL_LO:
                        n = KCH[k2][2]
                        dve.wait_ge(ph_ready, cnt(NCH, it, c2, k2 + 1))
                        nc.vector.tensor_tensor(pl[c2 % 2][:, POFF[k2]:POFF[k2] + n], p32[k2 % NRING][:, 0:n],
                                                ph[c2 % 2][:, POFF[k2]:POFF[k2] + n], ALU.subtract).then_inc(pl_ready, 1)
                    if k in (4, 11) and live(c - 1, it, c):
                        q = k // 11
                        dve.wait_ge(pv_done, cnt(2, it, c, -2 + q + 1))
                        o = O_BANK[q][:, 0:TB * VW].rearrange("p (i e) -> p i e", e=VW)
                        nc.vector.reciprocal(rsum[:, q, :], o[:, :, E]).then_inc(norm_done, 1)
                        dve.wait_ge(norm_done, cnt(4, it, c, -4 + 2 * q + 1))
                        half = slice(E * ((c - 1) // 2 % 2), E * ((c - 1) // 2 % 2) + E)
                        nc.vector.tensor_tensor(hpair[(c - 1) % 2][:, TB * q:TB * (q + 1), half], o[:, :, 0:E],
                                                rsum[:, q, :].unsqueeze(2).to_broadcast([P, TB, E]),
                                                ALU.mult).then_inc(norm_done, 1)
                    if k in WO_SLOTS and ends_pair(c - 2, it, c):
                        q = WO_SLOTS[k]
                        dve.wait_ge(wo_psum, pair_cnt(2, it, c - 2, q + 1))
                        dve.wait_ge(y_ready, pair_cnt(2, it, c - 2, q + 1))
                        t0 = QT * (c % 2) + TB * q
                        yv = acc[:, t0:t0 + TB, :].rearrange("p t d -> p (t d)")
                        nc.vector.tensor_tensor(yv, V_BANK[:, :], yv, ALU.add).then_inc(y_ready, 1)
                if live(c + 2, it, c):
                    dve.wait_ge(max_done, cnt(NCH, it, c, 3 * NCH))
                    wait_count(dve, mT_psum, cnt(1, it, c, 2))
                    nc.vector.tensor_reduce(negm[:, :], mpart[:, :, :], AX.X, ALU.max, negate=True).then_inc(mhl_ready, 1)
                    dve.wait_ge(mhl_ready, cnt(3, it, c, 7))
                    nc.vector.tensor_scalar(mhl[:, 0:QT], negm[:, :], 1.0 / M_UP, None, ALU.mult).then_inc(mhl_ready, 1)
                    dve.wait_ge(mhl_ready, cnt(3, it, c, 8))
                    nc.vector.scalar_tensor_tensor(mhl[:, QT:2 * QT], negm[:, :], 1.0 / M_UP, mhl[:, 0:QT],
                                                   ALU.mult, ALU.subtract).then_inc(mhl_ready, 1)
            run_periods(dve, period)
            dve.wait_ge(y_ready, NHEADS + 1)
            norm(2, acc, EPS_Y)
            dve.wait_ge(xn_ready, 3 * NT)
            dve.wait_ge(wo_in, 48)
            for t in range(NT):
                last = nc.vector.tensor_tensor(xn[:, t, :], xn[:, t, :], gam[:, :], ALU.mult)
            link(last)
            for t in range(NT):
                last = nc.vector.tensor_tensor(xn[:, t, :], xn[:, t, :], bet[:, :], ALU.add)
            link(last)
            for t in range(NT):
                last = nc.vector.tensor_tensor(res[:, t, :], res[:, t, :], xn[:, t, :], ALU.add)
                if t % TB == TB - 1:
                    last.then_inc(res_ready, 1)
            dve.wait_ge(res_ready, 2 * NBLK)
            norm(3, res, EPS)
            low_parts(2)
            ffn(1)

        @block.tensor
        def _(pe):
            def transposes(v, u):
                for g in range(NBLK):
                    if g >= 2:
                        pe.wait_ge(xh_ready, v * NBLK + g - 1)
                    for j in range(TB):
                        t = TB * g + j
                        pe.wait_ge(xn_ready, u * NT + t + 1)
                        last = nc.tensor.transpose(T_BANK[g % 2][:, j * P:(j + 1) * P], xn[:, t, :], identf[:, :])
                    last.then_inc(xT_psum, 1)

            def ffn(f, v):
                base = f * NEX * NBLK
                pe.wait_ge(xT_ready, (v + 1) * NBLK)
                pe.wait_ge(xh_ready, (v + 1) * NBLK)
                for t in range(NT):
                    last = nc.tensor.matmul(R_BANK[:, t * (NEX - 1):(t + 1) * (NEX - 1)], xT[:, t * P:(t + 1) * P],
                                            rw_sb[:, :], start=True, stop=True)
                last.then_inc(lg_psum, 1)

                def up(it, c, j):
                    e = c // NBLK if it is None else it + c // NBLK
                    wait_count(pe, hid_ready, cnt(FC, it, c, FC * (base - 1) + j + 1))
                    tok = slice((c % NBLK) * BLK, (c % NBLK + 1) * BLK)
                    wcol = bass.ds(e * F + j * P, P)
                    with kept_addresses():
                        nc.tensor.matmul(H_BANK[j][:, :], w1h[:, wcol], xh[:, tok], start=True, stop=False)
                        nc.tensor.matmul(H_BANK[j][:, :], w1h[:, wcol], xl[:, tok], start=False, stop=False)
                        nc.tensor.matmul(H_BANK[j][:, :], w1l[:, wcol], xh[:, tok], start=False,
                                         stop=True).then_inc(h_psum, 1)

                def down(it, c, j):
                    e = c // NBLK if it is None else it + c // NBLK
                    if j == 0:
                        wait_count(pe, acc_ready, cnt(TB, it, c, TB * (base - 1)))
                        pe.wait_ge(hid_ready, cnt(FC, it, c, FC * (base + 1)))
                    with kept_addresses():
                        for k in range(FC):
                            last = nc.tensor.matmul(Y_BANK[c % 2][:, j * P:(j + 1) * P], hid[c % 2][:, k, j * P:(j + 1) * P],
                                                    w2[:, bass.ds(e, 1), k, :], start=(k == 0), stop=(k == FC - 1))
                    last.then_inc(y_psum, 1)

                pe.wait_ge(xl_ready, (v + 1) * NBLK)
                if f == 0:
                    pe.wait_ge(wlo_ready, NEX)
                    pe.wait_ge(w2_in, 32)
                for j in range(FC):
                    up(None, 0, j)
                for s in (1, 2):
                    for j in range(FC):
                        up(None, s, j)
                        down(None, s - 1, j)
                with pe.Fori(0, NEX - 1) as it:
                    for c in range(3, 3 + NBLK):
                        for j in range(FC):
                            up(it, c, j)
                            down(it, c - 1, j)
                for s in range(NBLK * (NEX - 1) + 3, NBLK * NEX):
                    for j in range(FC):
                        up(None, s, j)
                        down(None, s - 1, j)
                for j in range(TB):
                    down(None, NBLK * NEX - 1, j)
                pe.wait_ge(comb_ready, f + 1)
                if f == 0:
                    pe.wait_ge(b_in, 64)
                for g in range(NBLK):
                    if g >= 2:
                        pe.wait_ge(cT_ready, f * NBLK + g - 1)
                    for j in range(TB):
                        last = nc.tensor.transpose(T_BANK[g % 2][0:NEX, j * P:(j + 1) * P], comb[:, TB * g + j, :], identf[:, :])
                    last.then_inc(cT_psum, 1)
                pe.wait_ge(hid_ready, FC * (base + NEX * NBLK))
                for g in range(NBLK):
                    pe.wait_ge(cT_ready, f * NBLK + g + 1)
                    for j in range(TB):
                        t = TB * g + j
                        last = nc.tensor.matmul(H_BANK[g][:, j * P:(j + 1) * P], combT[:, t * P:(t + 1) * P], b2[:, :],
                                                start=True, stop=True)
                    last.then_inc(b2_psum, 1)

            pe.wait_ge(const_ready, 1)
            pe.wait_ge(rw_in, 32)
            transposes(0, 0)
            ffn(0, 0)
            transposes(1, 1)
            pe.wait_ge(xl_ready, 2 * NBLK)
            pe.wait_ge(wlo_ready, NEX + 3)
            pe.wait_ge(b2_added, NBLK)
            pe.wait_ge(wo_in, 48)

            def period(it, c):
                m = c - 1
                waited = set()
                for k in range(NCH):
                    if live(c, it, c):
                        j, q0, n = KCH[k]
                        b = c % 4
                        if k == 0:
                            pe.wait_ge(stack_in, cnt(16 * 6, it, c, 16 * 6))
                            pe.wait_ge(mrow_in, cnt(16, it, c, 16))
                        wait_count(pe, exp_done, cnt(NCH, it, c, k - 1))
                        dst, keys = S_BANK[k % 2][:, 0:n], slice(j * P, (j + 1) * P)
                        nc.tensor.matmul(dst, ks[b][:, keys], qs[b][:, q0:q0 + n], start=True, stop=False)
                        nc.tensor.matmul(dst, km[b][:, keys], qm[b][:, q0:q0 + n], start=False,
                                         stop=True).then_inc(main_done, 1)
                    if live(c + 2, it, c):
                        i, k0, n = QCH[k]
                        b = (c + 2) % 4
                        if k == 0:
                            pe.wait_ge(stack_in, cnt(16 * 6, it, c, 3 * 16 * 6))
                        wait_count(pe, max_done, cnt(NCH, it, c, 2 * NCH + k - 1))
                        diag = k0 + n == P * (i + 1)
                        last = nc.tensor.matmul(A_BANK[k % 2][:, 0:n], qs[b][:, i * P:(i + 1) * P], ks[b][:, k0:k0 + n],
                                                start=True, stop=not diag)
                        if diag:
                            last = nc.tensor.matmul(A_BANK[k % 2][:, n - P:n], identb[:, :], tri[:, :],
                                                    start=False, stop=True)
                        last.then_inc(aux_done, 1)
                    if k == MT_SLOT and live(c + 1, it, c):
                        v = cnt(2, it, c, 8)
                        pe.wait_ge(lo_ready, min(v, 2 * NHEADS) if it is None else v)
                        pe.wait_ge(mhl_ready, cnt(3, it, c, 6))
                        nc.tensor.transpose(J_BANK[:, :].bitcast(f16)[0:2 * QT, 0:P], mhl[:, :],
                                            identh[:, :]).then_inc(mT_psum, 1)
                    if k in PROJ_SLOTS and live(c + 3, it, c):
                        g = PROJ_SLOTS[k]
                        wait_count(pe, lo_ready, cnt(2, it, c, 6 + g))
                        if g == 0:
                            wait_count(pe, mrows_ready, cnt(1, it, c, 1))
                        wcol = bass.ds(head_of(it, c + 3) * P, P)
                        t0 = ((c + 3) % 2) * S + 512 * g
                        with kept_addresses():
                            nc.tensor.matmul(J_BANK[:, :], wqk_h[:, wcol], xh[:, t0:t0 + 512], start=True, stop=False)
                            nc.tensor.matmul(J_BANK[:, :], wqk_h[:, wcol], xl[:, t0:t0 + 512], start=False, stop=False)
                            nc.tensor.matmul(J_BANK[:, :], wqk_l[:, wcol], xh[:, t0:t0 + 512], start=False,
                                             stop=True).then_inc(proj_done, 1)
                    if k in T_SLOTS and ends_pair(c - 2, it, c):
                        q = T_SLOTS[k]
                        if q == 0:
                            pe.wait_ge(norm_done, cnt(4, it, c, -4))
                            v = cnt(1, it, c, 1)
                            pe.wait_ge(v32_ready, min(v, NHEADS) if it is None else v)
                        else:
                            pe.wait_ge(hT_ready, pair_cnt(2, it, c - 2, 1))
                        for j in range(TB):
                            last = nc.tensor.transpose(V_BANK[:, j * P:(j + 1) * P], hpair[c % 2][:, TB * q + j, :],
                                                       identf[:, :])
                        last.then_inc(hT_psum, 1)
                    if k in WO_SLOTS and ends_pair(c - 2, it, c):
                        q = WO_SLOTS[k]
                        pe.wait_ge(hT_ready, pair_cnt(2, it, c - 2, 2))
                        if q == 1:
                            pe.wait_ge(y_ready, pair_cnt(2, it, c - 2, 2))
                        pair = (c - 2) // 4 if it is None else it + (c - 2) // 4
                        with kept_addresses():
                            for j in range(TB):
                                last = nc.tensor.matmul(V_BANK[:, j * P:(j + 1) * P], hpT[q][:, j * P:(j + 1) * P],
                                                        wo_sb[:, bass.ds(pair, 1), :], start=True, stop=True)
                        last.then_inc(wo_psum, 1)
                    if k == V_SLOT and live(c + 1, it, c):
                        if ends_pair(c - 2, it, c):
                            pe.wait_ge(y_ready, pair_cnt(2, it, c - 2, 3))
                        wait_count(pe, v32_ready, cnt(1, it, c, 1))
                        wv = bass.ds(head_of(it, c + 1) * E, E)
                        with kept_addresses():
                            for j in range(QT):
                                tok = slice(((c + 1) % 2) * S + j * P, ((c + 1) % 2) * S + (j + 1) * P)
                                dst = V_BANK[:, j * E:(j + 1) * E]
                                nc.tensor.matmul(dst, xh[:, tok], wv_h[:, wv], start=True, stop=False)
                                nc.tensor.matmul(dst, xh[:, tok], wv_l[:, wv], start=False, stop=False)
                                last = nc.tensor.matmul(dst, xl[:, tok], wv_h[:, wv], start=False, stop=True)
                        last.then_inc(v_psum, 1)
                    if live(m, it, c):
                        for i, j in BLOCKS[BPS * k:BPS * (k + 1)]:
                            q = i // TB
                            if (i, j) == (0, 0):
                                pe.wait_ge(vl_ready, cnt(1, it, c, 0))
                            if j == 0 and i % TB == 0:
                                wait_count(pe, norm_done, cnt(4, it, c, -8 + 2 * q + 2))
                            ch = KIDX[(j, q)]
                            if ch not in waited:
                                wait_split(pe, it, m, ch)
                            waited.add(ch)
                            cols = slice(POFF[ch] + i * P - KCH[ch][1], POFF[ch] + i * P - KCH[ch][1] + P)
                            o = O_BANK[q][:, (i % TB) * VW:(i % TB + 1) * VW]
                            nc.tensor.matmul(o, ph[m % 2][:, cols], vh[m % 4][:, j, :], start=(j == 0), stop=False)
                            nc.tensor.matmul(o[:, 0:E], ph[m % 2][:, cols], vl[m % 4][:, j, :], start=False, stop=False)
                            last = nc.tensor.matmul(o, pl[m % 2][:, cols], vh[m % 4][:, j, :], start=False, stop=(j == i))
                            if i == j and i % TB == TB - 1:
                                last.then_inc(pv_done, 1)
            run_periods(pe, period)

            transposes(2, 3)
            ffn(1, 2)


def kernel(L0_attn_x, L0_attn_Wq, L0_attn_Wk, L0_attn_Wv, L0_attn_Wo, L0_attn_gamma, L0_attn_beta,
           L0_ffn_shared_w1, L0_ffn_shared_b1, L0_ffn_shared_w2, L0_ffn_shared_b2, L0_ffn_router_w, L0_ffn_router_b,
           L0_ffn_spec_w1, L0_ffn_spec_b1, L0_ffn_spec_w2, L0_ffn_spec_b2):
    import numpy as np
    import concourse.bacc as bacc
    from concourse.bass_utils import run_bass_kernel_spmd

    P = 128
    B, S, D = L0_attn_x.shape
    NEX, F, _ = L0_ffn_spec_w1.shape
    NT, FC = B * S // P, F // P
    laid = {
        "x": L0_attn_x.reshape(NT, P, D).transpose(1, 0, 2),
        "w1s": L0_ffn_shared_w1.T,
        "w1e": L0_ffn_spec_w1.transpose(2, 0, 1),
        "w2s": L0_ffn_shared_w2.T.reshape(FC, P, D).transpose(1, 0, 2),
        "w2e": L0_ffn_spec_w2.transpose(2, 0, 1).reshape(FC, P, NEX, D).transpose(1, 2, 0, 3),
        "b1s": L0_ffn_shared_b1.reshape(FC, P).T,
        "b1e": L0_ffn_spec_b1.reshape(NEX, FC, P).transpose(2, 0, 1),
        "b2s": L0_ffn_shared_b2.reshape(1, D),
        "b2e": L0_ffn_spec_b2,
        "rw": L0_ffn_router_w.T,
        "rb": L0_ffn_router_b,
        "wq": L0_attn_Wq.transpose(1, 0, 2),
        "wk": L0_attn_Wk.transpose(1, 0, 2),
        "wv": L0_attn_Wv.transpose(1, 0, 2),
        "wo": L0_attn_Wo.reshape(-1, P, D).transpose(1, 0, 2),
        "gamma": L0_attn_gamma,
        "beta": L0_attn_beta,
    }
    nc = bacc.Bacc("TRN2", target_bir_lowering=False, num_devices=1)
    arrays = {n: np.ascontiguousarray(a) for n, a in laid.items()}
    args = [nc.dram_tensor(n, a.shape, mybir.dt.from_np(a.dtype), kind="ExternalInput").ap() for n, a in arrays.items()]
    out = nc.dram_tensor("out", (P, NT, D), mybir.dt.float32, kind="ExternalOutput").ap()
    macaron_block_kernel(nc, *args, out)
    r = run_bass_kernel_spmd(nc, [arrays], core_ids=[0])
    y = r.results[0]["out"]
    return y.transpose(1, 0, 2).reshape(B, S, D)
```

```python
import concourse.bass as bass
from concourse import mybir
from contextlib import ExitStack, contextmanager


def macaron_block_kernel(nc, x, w1s, w1e, w2s, w2e, b1s, b1e, b2s, b2e, rw, rb, wq, wk, wv, wo, gamma, beta, out):
    f32, f16, bf16, i32 = mybir.dt.float32, mybir.dt.float16, mybir.dt.bfloat16, mybir.dt.int32
    ALU, ACT, AX = mybir.AluOpType, mybir.ActivationFunctionType, mybir.AxisListType

    P = 128
    D = x.shape[2]
    NT = x.shape[1]
    S = 1024
    NB = NT * P // S
    QT = S // P
    E = wq.shape[2]
    NH = wq.shape[1]
    NEX = w1e.shape[1] + 1
    NR = NEX - 1
    F = w1e.shape[2]
    FC = F // P
    TB = 4
    NBLK = NT // TB
    BLK = TB * P
    EPS, EPS_Y = 1e-5, 1e-3
    W1_UP = 64.0
    WA_UP = 16.0
    M_UP = 64.0
    B2_UP = 2 * W1_UP * W1_UP
    NEG = -1e30
    SCALE = float(E) ** -0.5
    NHEADS = NB * NH
    VW = E + 1
    PAIRS = NH * E // P

    KCH = [(j, P * j, 512 - P * j) for j in range(4)] + [(j, 512, 512) for j in range(4)] + \
          [(j, P * j, S - P * j) for j in range(4, QT)]
    NCH = len(KCH)
    POFF = [sum(c[2] for c in KCH[:k]) for k in range(NCH)]
    PW = sum(c[2] for c in KCH)
    KIDX = {(j, 0 if q0 < 512 else 1): k for k, (j, q0, n) in enumerate(KCH)}
    DIAG = [k for k, (j, q0, n) in enumerate(KCH) if q0 == P * j]
    by_width = {}
    for ch in [(i, 0, P * (i + 1)) for i in range(4)] + \
            [c for i in range(4, QT) for c in ((i, 0, 512), (i, 512, P * (i + 1) - 512))]:
        by_width.setdefault(ch[2], []).append(ch)
    QCH = [by_width[n].pop() for n in (512, 512, 384, 256, 512, 512, 128, 256, 512, 384, 512, 128)]
    assert len(QCH) == NCH and not any(by_width.values())
    BLOCKS = [(i, j) for i in range(QT) for j in range(i + 1)]
    BPS = len(BLOCKS) // NCH
    POOL_LO = [2, 5, 7, 9]
    MT_SLOT = 6
    PROJ_SLOTS = {0: 0, 3: 1}
    T_SLOTS = {1: 0, 3: 1}
    WO_SLOTS = {5: 0, 8: 1}
    V_SLOT = 10

    COMB_STEP = 0
    CT_STEP = 6
    POST_STAT, POST_NORM, POST_T = 1, 1, 4
    PEEL = 5, 2
    Y_STAT, Y_NORM = 2, 3
    PRE_STEPS = (5, 5), (4, 5)
    PRE_T, ROUTE = 7, 8
    SPLIT_AT = {0: (2,), 1: (3,), 2: (4,), 3: (5, 6), 4: (7, 8)}
    NEWTON = 3
    LAG = 2
    HRING = LAG + 1

    nc.disable_value_cache = True

    @contextmanager
    def kept_addresses():
        nc.disable_value_cache = False
        yield
        nc.disable_value_cache = True

    ctx = ExitStack()
    with ctx:
        def sb(name, shape, dt=f32):
            return ctx.enter_context(nc.sbuf_tensor(name, shape, dt))

        def sem(name):
            return ctx.enter_context(nc.semaphore(name))

        bank = [ctx.enter_context(nc.psum_tensor(f"bank{i}", [P, 512], f32)) for i in range(8)]

        res = sb("res", [P, NT, D])
        acc = sb("acc", [P, NT, D])
        res2, acc2 = (t[:, :, :].rearrange("p t d -> p (t d)") for t in (res, acc))
        xn = sb("xn", [P, TB, D])
        xa = sb("xa", [P, TB, D])
        xT = sb("xT", [P, BLK])
        xh = sb("xh", [P, NT * P], f16)
        xl = sb("xl", [P, NT * P], f16)
        stats = sb("stats", [P, TB, 6])
        mv = sb("mv", [P, TB, 2])
        veps = sb("veps", [P, TB])
        rstd = sb("rstd", [P, TB])
        corr = sb("corr", [P, TB])
        half = sb("half", [P, TB], i32)
        w1h = sb("w1h", [P, NEX * F], f16)
        w1l = sb("w1l", [P, NEX * F], f16)
        w2h = sb("w2h", [P, NEX, FC * D], f16)
        w2l = sb("w2l", [P, NEX, FC * D], f16)
        b1 = sb("b1", [P, NEX * FC])
        b2 = sb("b2", [NEX, D])
        rw_sb = sb("rw_sb", [P, NEX - 1])
        rb_sb = sb("rb_sb", [P, NEX - 1])
        wqk_h = sb("wqk_h", [P, NH * 2 * E], f16)
        wqk_l = sb("wqk_l", [P, NH * 2 * E], f16)
        wqk_h4, wqk_l4 = (w[:, :].rearrange("p (h i e) -> p h i e", i=2, h=NH) for w in (wqk_h, wqk_l))
        wv_h = sb("wv_h", [P, NH * E], f16)
        wv_l = sb("wv_l", [P, NH * E], f16)
        wo_sb = sb("wo_sb", [P, PAIRS, D])
        gam = sb("gam", [P, D])
        bet = sb("bet", [P, D])
        identf = sb("identf", [P, P])
        identh = sb("identh", [P, P], f16)
        identb = sb("identb", [P, P], bf16)
        tri = sb("tri", [P, P], bf16)
        rev = sb("rev", [P, NEX - 1])
        lg = sb("lg", [P, TB, NR])
        lg2 = sb("lg2", [P, TB, NR])
        rk = sb("rk", [P, TB, NR])
        sel = [sb(f"sel{i}", [P, TB, NR]) for i in range(2)]
        top = [sb(f"top{i}", [P, TB]) for i in range(2)]
        wgt = [sb(f"wgt{i}", [P, TB]) for i in range(2)]
        first = sb("first", [P, TB])
        diff = sb("diff", [P, TB])
        tanh = sb("tanh", [P, TB])
        comb = sb("comb", [P, TB, NEX])
        probs = [sb(f"probs{i}", [P, 2 * PW], f16) for i in range(2)]
        ph = [t[:, 0:PW] for t in probs]
        pl = [t[:, PW:2 * PW] for t in probs]
        NRING = 6
        p32 = [sb(f"p32_{i}", [P, 512]) for i in range(NRING)]
        hh = [sb(f"hh{i}", [P, S], f16) for i in range(2)]
        ll = [sb(f"ll{i}", [P, S], f16) for i in range(2)]
        qsks = sb("qsks", [P, 8 * S], f16)
        qs = [qsks[:, i * S:(i + 1) * S] for i in range(4)]
        ks = [qsks[:, (4 + i) * S:(5 + i) * S] for i in range(4)]
        qms = sb("qms", [E + 2, 4 * S], f16)
        qm = [qms[:, i * S:(i + 1) * S] for i in range(4)]
        km = [sb(f"km{i}", [E + 2, S], f16) for i in range(4)]
        vh = [sb(f"vh{i}", [P, QT, VW], f16) for i in range(4)]
        vl = [sb(f"vl{i}", [P, QT, E], f16) for i in range(4)]
        v32 = [sb(f"v32_{i}", [P, QT, E]) for i in range(2)]
        hpair = [sb(f"hpair{i}", [P, QT, 2 * E]) for i in range(NB)]
        hpT = [sb(f"hpT{i}", [P, BLK]) for i in range(2)]
        stage = probs[0][:, :].bitcast(f32)[:, 0:NEX * F]
        hid = [qsks[:, i * FC * BLK:(i + 1) * FC * BLK] for i in range(4)] + \
              [t[:, :, :].rearrange("p t e -> p (t e)").bitcast(f16) for t in hpair]
        hid = [t.rearrange("p (c n) -> p c n", c=FC) for t in hid]
        hidh, hidl = [hid[0], hid[1], hid[4]], [hid[2], hid[3], hid[5]]
        stage2 = [probs[1][:, :].bitcast(f32)[:, e * FC * D:(e + 1) * FC * D] for e in range(NEX)]
        combT = qms[:, :].bitcast(f32)[0:NEX, 0:BLK]
        h32 = [t[:, :] for t in p32] + [t[:, :, :].rearrange("p t e -> p (t e)") for t in v32] + \
              [t[:, :].bitcast(f32) for t in hh + ll]
        mpart = sb("mpart", [P, QT, 2])
        negm = sb("negm", [P, QT])
        mhl = sb("mhl", [P, 2 * QT], f16)
        mrows = sb("mrows", [2 * QT, P], f16)
        rsum = sb("rsum", [P, 2, TB])

        S_BANK, A_BANK, O_BANK, J_BANK, V_BANK = bank[0:2], bank[2:4], bank[4:6], bank[6], bank[7]
        H_BANK, Y_BANK, T_BANK = bank[0:4], bank[4:7], bank[7]

        x_in = [sem(f"x_in{g}") for g in range(NBLK)]
        w1_in = [sem(f"w1_in{e}") for e in range(NEX)]
        w2_in = [sem(f"w2_in{e}") for e in range(NEX)]
        rw_in, b1_in, b2_in, wa_in, wo_in, out_done = (sem(n) for n in
            ("rw_in", "b1_in", "b2_in", "wa_in", "wo_in", "out_done"))
        const_ready, const2_ready, w_hi = sem("const_ready"), sem("const2_ready"), sem("w_hi")
        w1_ready, w2_dve, w2_pool, b2_scaled, wa_ready = (sem(n) for n in
            ("w1_ready", "w2_dve", "w2_pool", "b2_scaled", "wa_ready"))
        pre_step, post_step, y_step, router_step, weight_step = (sem(n) for n in
            ("pre_step", "post_step", "y_step", "router_step", "weight_step"))
        pre_xn, pre_T, pre_xT, pre_xh = (sem(n) for n in ("pre_xn", "pre_T", "pre_xT", "pre_xh"))
        post_xn, post_T, post_xh, xa_free = (sem(n) for n in ("post_xn", "post_T", "post_xh", "xa_free"))
        beta_added, y_scaled, y_added = sem("beta_added"), sem("y_scaled"), sem("y_added")
        lg_psum, tanh_ready, comb_ready, cT_psum = (sem(n) for n in ("lg_psum", "tanh_ready", "comb_ready", "cT_psum"))
        t_read = sem("t_read")
        h_psum, h32_ready, hidh_ready, hidl_ready, y_psum, acc_ready = (sem(n) for n in
            ("h_psum", "h32_ready", "hidh_ready", "hidl_ready", "y_psum", "acc_ready"))
        v_psum = sem("v_psum")
        proj_done, hi_ready, lo_ready, stack_in = sem("proj_done"), sem("hi_ready"), sem("lo_ready"), sem("stack_in")
        ph_ready, pl_ready, pool_lo_ready = sem("ph_ready"), sem("pl_ready"), sem("pool_lo_ready")
        v32_ready, vl_ready = sem("v32_ready"), sem("vl_ready")
        aux_done, max_done, mhl_ready, mT_psum, mrows_ready, mrow_in = (sem(n) for n in
            ("aux_done", "max_done", "mhl_ready", "mT_psum", "mrows_ready", "mrow_in"))
        main_done, exp_done, mask_done, pv_done, norm_done = (sem(n) for n in
            ("main_done", "exp_done", "mask_done", "pv_done", "norm_done"))
        hT_psum, hT_ready, wo_psum, y_ready = sem("hT_psum"), sem("hT_ready"), sem("wo_psum"), sem("y_ready")
        pool_step = sem("pool_step")

        def scnt(per, f, it, c, plus=0):
            n = per * (f * NEX * NBLK + c) + plus
            return n if it is None else it * (per * NEX) + n

        def bcnt(per, f, it, b, plus=0):
            n = per * (f * NBLK + b) + plus
            return n if it is None else it * per + n

        def t_uses(f, it, b, use):
            per = 3 if f else 4
            if use in ("pre", "route"):
                n = (3 + per * (b - 1) if it is not None or b > 0 else 0) + (use == "route")
            elif use == "comb":
                n = 2 + per * b
            else:
                n = 5 + per * b if it is not None or b + 1 < NBLK else 3 + per * b
            n += f * (4 * NBLK)
            return n if it is None else it * per + n

        def block_cols(it, b):
            return slice(b * BLK, (b + 1) * BLK) if it is None else bass.ds(it * BLK + b * BLK, BLK)

        def tile_cols(it, t):
            return slice(t * D, (t + 1) * D) if it is None else bass.ds(it * (TB * D) + t * D, D)

        def run_steps(eng, f, step):
            for s in range(PEEL[f]):
                step(None, s)
            with eng.Fori(0, NBLK - 1) as it:
                for c in range(PEEL[f], PEEL[f] + NEX):
                    step(it, c)
            for s in range(PEEL[f] + NEX * (NBLK - 1), NEX * NBLK):
                step(None, s)

        STAT_STEPS, ROUTER_STEPS, WEIGHT_STEPS = 5 + 3 * NEWTON, 12, 2

        def has_next(it, c):
            return it is not None or c // NEX + 1 < NBLK

        def head_of(it, c):
            return it * 2 + c // 2 if it is not None else c // 2

        def cnt(per, it, c, plus=0):
            return per * c + plus if it is None else it * (4 * per) + (per * c + plus)

        def wait_count(eng, s, v):
            if not isinstance(v, int) or v > 0:
                eng.wait_ge(s, v)

        def pair_cnt(per, it, c, plus=0):
            done = 2 * (c // 4) + (c % 2)
            return per * done + plus if it is None else it * (2 * per) + (per * done + plus)

        def wait_split(eng, it, c, k):
            while k < 0:
                c, k = c - 1, k + NCH
            if k in POOL_LO:
                wait_count(eng, pool_lo_ready, cnt(len(POOL_LO), it, c, POOL_LO.index(k) + 1))
            else:
                before = len([j for j in range(k) if j not in POOL_LO])
                wait_count(eng, pl_ready, cnt(NCH - len(POOL_LO), it, c, before + 1))

        def ends_pair(n, it, c):
            return live(n, it, c) and n % 4 >= 2

        def live(n, it, c):
            return it is not None or 0 <= n < NHEADS

        EARLY = (-3, -2)
        FIRST = 2
        LAST = FIRST + (NHEADS - 3 - FIRST) // 4 * 4 - 1

        def projects(it, c):
            return live(c + 3, it, c) and (it is not None or c > EARLY[-1])

        def pair_banks(it, c, q):
            if it is None and c == NHEADS + 1:
                return S_BANK[q], A_BANK[q]
            return V_BANK, V_BANK

        def run_periods(eng, period, before_last=lambda: None):
            for t in range(-3, FIRST):
                period(None, t)
            with eng.Fori(0, (LAST + 1 - FIRST) // 4) as it:
                for c in range(FIRST, FIRST + 4):
                    period(it, c)
            for t in range(LAST + 1, NHEADS + 2):
                if t == NHEADS + 1:
                    before_last()
                period(None, t)

        block = ctx.enter_context(nc.Block())

        @block.sync
        def _(sp):
            def tokens(g):
                sp.dma_start(res[:, TB * g:TB * (g + 1), :], x[:, TB * g:TB * (g + 1), :]).then_inc(x_in[g], 16)

            def weights(e):
                w1, w2 = (w1s, w2s) if e == NR else (w1e[:, e], w2e[:, e])
                sp.dma_start(stage[:, e * F:(e + 1) * F], w1).then_inc(w1_in[e], 16)
                sp.dma_start(stage2[e], w2.rearrange("p c d -> p (c d)")).then_inc(w2_in[e], 16)
            tokens(0)
            sp.dma_start(rw_sb[:, :], rw).then_inc(rw_in, 16)
            sp.dma_start(rb_sb[:, :], rb.partition_broadcast(P)).then_inc(rw_in, 16)
            weights(0)
            sp.dma_start(b1[:, 0:NR * FC], b1e.rearrange("p e f -> p (e f)")).then_inc(b1_in, 16)
            sp.dma_start(b1[:, NR * FC:], b1s).then_inc(b1_in, 16)
            weights(1)
            weights(2)
            tokens(1)
            for e in range(3, NEX):
                weights(e)
            sp.dma_start(b2[0:NR, :], b2e).then_inc(b2_in, 16)
            sp.dma_start(b2[NR:NEX, :], b2s).then_inc(b2_in, 16)
            for g in range(2, NBLK):
                tokens(g)
            sp.dma_start(gam[:, :], gamma.partition_broadcast(P)).then_inc(wo_in, 16)
            sp.dma_start(bet[:, :], beta.partition_broadcast(P)).then_inc(wo_in, 16)
            sp.dma_start(wo_sb[:, :, :], wo).then_inc(wo_in, 16)
            sp.wait_ge(w1_ready, NEX)
            for i, w in enumerate((wq, wk, wv)):
                sp.dma_start(stage[:, i * NH * E:(i + 1) * NH * E], w.rearrange("p h e -> p (h e)")).then_inc(wa_in, 16)

            def period(it, c):
                if live(c + 3, it, c):
                    b, r = (c + 3) % 4, (c + 3) % 2
                    wait_count(sp, main_done, cnt(NCH, it, c, 0))
                    wait_count(sp, stack_in, cnt(16 * 6, it, c, 3 * 16 * 6))
                    sp.wait_ge(hi_ready, cnt(2, it, c, 8))
                    sp.dma_start(qs[b][0:E, :], hh[r][0:E, :]).then_inc(stack_in, 16)
                    sp.dma_start(qm[b][0:E, :], hh[r][0:E, :]).then_inc(stack_in, 16)
                    sp.dma_start(ks[b][0:E, :], hh[r][E:P, :]).then_inc(stack_in, 16)
                    sp.dma_start(ks[b][E:P, :], hh[r][E:P, :]).then_inc(stack_in, 16)
                    sp.wait_ge(lo_ready, cnt(2, it, c, 8))
                    sp.dma_start(qs[b][E:P, :], ll[r][0:E, :]).then_inc(stack_in, 16)
                    sp.dma_start(km[b][0:E, :], ll[r][E:P, :]).then_inc(stack_in, 16)
                if live(c + 1, it, c):
                    sp.wait_ge(mrows_ready, cnt(1, it, c, 2))
                    sp.dma_start(qm[(c + 1) % 4][E:E + 2, :].rearrange("r (i q) -> r i q", i=QT),
                                 mrows[:, :]).then_inc(mrow_in, 16)
            run_periods(sp, period)
            for g in range(NBLK):
                sp.wait_ge(acc_ready, scnt(TB, 1, None, NEX * (g + 1)))
                sp.dma_start(out[:, TB * g:TB * (g + 1), :], res[:, TB * g:TB * (g + 1), :]).then_inc(out_done, 16)
            sp.wait_ge(out_done, 16 * NBLK)

        @block.gpsimd
        def _(pool):
            steps = [0]

            def link(ins):
                steps[0] += 1
                ins.then_inc(pool_step, 1)
                pool.wait_ge(pool_step, steps[0])

            def identity(t):
                link(nc.gpsimd.memset(t[:, :], 0.0))
                return nc.gpsimd.affine_select(out=t[:, :], in_=t[:, :], compare_op=ALU.not_equal, fill=1.0, base=0,
                                               pattern=[[-1, P]], channel_multiplier=1)
            link(identity(identf))
            pool.nop().then_inc(xa_free, 1)
            for e in range(NR):
                link(nc.gpsimd.memset(rev[:, e:e + 1], float(NR - e)))
            nc.gpsimd.memset(comb[:, :, NR:NEX], 0.5 / W1_UP).then_inc(const_ready, 1)

            for e in range(1, NEX):
                pool.wait_ge(w_hi, 2 * e + 2)
                link(nc.gpsimd.tensor_scalar(stage2[e], stage2[e], W1_UP, None, ALU.mult))
                nc.gpsimd.tensor_tensor(w2l[:, e, :], stage2[e], w2h[:, e, :], ALU.subtract).then_inc(w2_pool, 1)
            pool.wait_ge(b2_in, 32)
            nc.gpsimd.tensor_scalar(b2[:, :], b2[:, :], B2_UP, None, ALU.mult).then_inc(b2_scaled, 1)
            link(identity(identh))
            link(identity(identb))
            link(nc.gpsimd.memset(tri[:, :], 0.0))
            link(nc.gpsimd.affine_select(out=tri[:, :], in_=tri[:, :], compare_op=ALU.is_ge, fill=NEG, base=0,
                                         pattern=[[-1, P]], channel_multiplier=1))
            for i in range(4):
                link(nc.gpsimd.memset(km[i][E:E + 2, :], M_UP))
            nc.gpsimd.memset(mpart[:, :, :], -3e38)
            for i in range(3):
                nc.gpsimd.memset(vh[i][:, :, E:VW], 1.0)
            nc.gpsimd.memset(vh[3][:, :, E:VW], 1.0).then_inc(const2_ready, 1)
            pool.wait_ge(wa_in, 48)
            NE = NH * E
            link(nc.gpsimd.tensor_scalar(stage[:, 0:3 * NE], stage[:, 0:3 * NE], WA_UP, None, ALU.mult))
            for i in range(2):
                src = stage[:, i * NE:(i + 1) * NE].rearrange("p (h e) -> p h e", e=E)
                link(nc.gpsimd.tensor_copy(wqk_h4[:, :, i, :], src))
                nc.gpsimd.tensor_tensor(wqk_l4[:, :, i, :], src, wqk_h4[:, :, i, :], ALU.subtract).then_inc(wa_ready, 1)
            link(nc.gpsimd.tensor_copy(wv_h[:, :], stage[:, 2 * NE:3 * NE]))
            nc.gpsimd.tensor_tensor(wv_l[:, :], stage[:, 2 * NE:3 * NE], wv_h[:, :], ALU.subtract).then_inc(wa_ready, 1)

            pool.wait_ge(wo_in, 48)
            for g in range(NBLK):
                pool.wait_ge(post_xn, TB * (g + 1))
                nc.gpsimd.tensor_copy(acc[:, TB * g:TB * (g + 1), :], xa[:, :, :]).then_inc(xa_free, 1)
                rv = res[:, TB * g:TB * (g + 1), :]
                nc.gpsimd.tensor_tensor(rv, rv, bet[:, :].unsqueeze(1).to_broadcast([P, TB, D]),
                                        ALU.add).then_inc(beta_added, 1)

            def period(it, c):
                if live(c, it, c):
                    for _, split, k in sorted([(k, False, k) for k in DIAG] + [(k + 1, True, k) for k in POOL_LO]):
                        if split:
                            n = KCH[k][2]
                            pool.wait_ge(ph_ready, cnt(NCH, it, c, k + 1))
                            nc.gpsimd.tensor_tensor(pl[c % 2][:, POFF[k]:POFF[k] + n], p32[k % NRING][:, 0:n],
                                                    ph[c % 2][:, POFF[k]:POFF[k] + n],
                                                    ALU.subtract).then_inc(pool_lo_ready, 1)
                            continue
                        pool.wait_ge(exp_done, cnt(NCH, it, c, k + 1))
                        pool.nop(nofuse=True)
                        d = p32[k % NRING][:, 0:P]
                        nc.gpsimd.affine_select(out=d, in_=d, compare_op=ALU.is_ge, fill=0.0, base=0,
                                                pattern=[[1, P]], channel_multiplier=-1).then_inc(mask_done, 1)
                if live(c + 1, it, c):
                    pool.wait_ge(v32_ready, cnt(1, it, c, 2))
                    nc.gpsimd.tensor_tensor(vl[(c + 1) % 4][:, :, :], v32[(c + 1) % 2][:, :, :],
                                            vh[(c + 1) % 4][:, :, 0:E], ALU.subtract).then_inc(vl_ready, 1)
            run_periods(pool, period)
        @block.scalar
        def _(act):
            def evacuate_pre(f, it, b):
                act.wait_ge(pre_T, bcnt(1, f, it, b, 1))
                act.nop(nofuse=True)
                nc.scalar.copy(xT[:, :], T_BANK[:, :]).then_inc(pre_xT, 1)
                nc.scalar.copy(xh[:, block_cols(it, b)], T_BANK[:, :]).then_inc(pre_xh, 1)

            def evacuate_post(it, b):
                act.wait_ge(post_T, bcnt(1, 0, it, b, 1))
                act.nop(nofuse=True)
                nc.scalar.copy(xh[:, block_cols(it, b)], T_BANK[:, :]).then_inc(post_xh, 1)

            def split_hi(e, first=True, second=True):
                if first:
                    act.wait_ge(w1_in[e], 16)
                    nc.scalar.mul(w1h[:, e * F:(e + 1) * F], stage[:, e * F:(e + 1) * F], W1_UP).then_inc(w_hi, 1)
                if second:
                    act.wait_ge(w2_in[e], 16)
                    nc.scalar.mul(w2h[:, e, :], stage2[e], W1_UP).then_inc(w_hi, 1)

            def ffn(f):
                def step(it, c):
                    e, b = c % NEX, c // NEX
                    buf = e % HRING

                    def gelu(j):
                        slot = (FC * e + j) % len(h32)
                        act.wait_ge(h_psum, scnt(FC, f, it, c, j + 1))
                        wait_count(act, hidl_ready, scnt(FC, f, it, c, j + 1 - len(h32)))
                        act.nop(nofuse=True)
                        nc.scalar.activation(h32[slot], H_BANK[j][:, :], ACT.Gelu_apprx_tanh,
                                             bias=b1[:, e * FC + j:e * FC + j + 1],
                                             scale=1.0 / W1_UP).then_inc(h32_ready, 1)

                    def hi(j):
                        slot = (FC * e + j) % len(h32)
                        act.wait_ge(h32_ready, scnt(FC, f, it, c, j + 1))
                        wait_count(act, y_psum, scnt(TB, f, it, c, -TB * (HRING - 1)))
                        nc.scalar.copy(hidh[buf][:, j, :], h32[slot]).then_inc(hidh_ready, 1)
                    gelu(0)
                    for j in range(1, FC):
                        gelu(j)
                        hi(j - 1)
                    hi(FC - 1)
                    if f == 0 and it is None:
                        for expert in SPLIT_AT.get(c, ()):
                            split_hi(expert)
                    if e == COMB_STEP:
                        act.wait_ge(router_step, bcnt(ROUTER_STEPS, f, it, b, ROUTER_STEPS))
                        nc.scalar.activation(tanh[:, :], diff[:, :], ACT.Tanh, scale=0.5).then_inc(tanh_ready, 1)
                    if e == CT_STEP:
                        act.wait_ge(cT_psum, bcnt(1, f, it, b, 1))
                        nc.scalar.copy(combT, T_BANK[0:NEX, :]).then_inc(t_read, 1)
                    if e == POST_T and f == 0 and (it is not None or b > 0):
                        evacuate_post(it, b - 1)
                    if e == PRE_T and has_next(it, c):
                        evacuate_pre(f, it, b + 1)
                run_steps(act, f, step)

            def project_hi(it, c, g):
                act.wait_ge(proj_done, cnt(2, it, c, 6 + g + 1))
                if g == 0:
                    wait_count(act, stack_in, cnt(16 * 6, it, c, 2 * 16 * 6))
                nc.scalar.mul(hh[(c + 3) % 2][:, 512 * g:512 * g + 512], J_BANK[:, :],
                              1.0 / WA_UP).then_inc(hi_ready, 1)

            split_hi(0, second=False)
            evacuate_pre(0, None, 0)
            split_hi(0, first=False)
            split_hi(1)
            act.wait_ge(b1_in, 32)
            ffn(0)
            for g in range(2):
                project_hi(None, EARLY[0], g)
            evacuate_post(None, NBLK - 1)
            for g in range(2):
                project_hi(None, EARLY[1], g)

            def period(it, c):
                for k in range(NCH):
                    if k - 1 in PROJ_SLOTS and projects(it, c):
                        project_hi(it, c, PROJ_SLOTS[k - 1])
                    if live(c, it, c):
                        j, q0, n = KCH[k]
                        act.wait_ge(main_done, cnt(NCH, it, c, k + 1))
                        wait_split(act, it, c, k - NRING)
                        nc.scalar.activation(p32[k % NRING][:, 0:n], S_BANK[k % 2][:, 0:n], ACT.Exp,
                                             scale=SCALE).then_inc(exp_done, 1)
                    k1, c1 = (k - 1) % NCH, c if k >= 1 else c - 1
                    if live(c1, it, c):
                        n = KCH[k1][2]
                        if k1 in DIAG:
                            act.wait_ge(mask_done, cnt(8, it, c1, DIAG.index(k1) + 1))
                        else:
                            act.wait_ge(exp_done, cnt(NCH, it, c1, k1 + 1))
                        if k1 == 0:
                            wait_count(act, pv_done, cnt(2, it, c, -2))
                        nc.scalar.copy(ph[c1 % 2][:, POFF[k1]:POFF[k1] + n], p32[k1 % NRING][:, 0:n]).then_inc(ph_ready, 1)
                    if k == MT_SLOT + 1 and live(c + 1, it, c):
                        act.wait_ge(mT_psum, cnt(1, it, c, 2))
                        wait_count(act, mrow_in, cnt(16, it, c, 16))
                        nc.scalar.copy(mrows[:, :], J_BANK[:, :].bitcast(f16)[0:2 * QT, 0:P]).then_inc(mrows_ready, 1)
                    if k in T_SLOTS and ends_pair(c - 2, it, c):
                        q = T_SLOTS[k]
                        act.wait_ge(hT_psum, pair_cnt(2, it, c - 2, q + 1))
                        nc.scalar.copy(hpT[q][:, :], pair_banks(it, c, q)[0][:, :]).then_inc(hT_ready, 1)
                    if k == V_SLOT and live(c + 1, it, c):
                        act.wait_ge(v_psum, cnt(1, it, c, 2))
                        nc.scalar.mul(vh[(c + 1) % 4][:, :, 0:E], V_BANK[:, :].rearrange("p (t e) -> p t e", e=E),
                                      1.0 / WA_UP)
                        wait_count(act, vl_ready, cnt(1, it, c, 0))
                        nc.scalar.mul(v32[(c + 1) % 2][:, :, :], V_BANK[:, :].rearrange("p (t e) -> p t e", e=E),
                                      1.0 / WA_UP).then_inc(v32_ready, 1)
            run_periods(act, period)
            evacuate_pre(1, None, 0)
            ffn(1)

        @block.vector
        def _(dve):
            def chain(s, per, f, it, b):
                done = [0]

                def link(ins):
                    done[0] += 1
                    ins.then_inc(s, 1)
                    dve.wait_ge(s, bcnt(per, f, it, b, done[0]))
                return link

            def statistics(link, src, it, b, eps):
                for j in range(TB):
                    last = nc.vector.bn_stats(stats[:, j, :], src[:, tile_cols(it, TB * b + j)])
                link(last)
                dve.nop(nofuse=True)
                for j in range(TB):
                    last = nc.vector.bn_aggr(mv[:, j, :], stats[:, j, :])
                link(last)
                link(nc.vector.tensor_scalar(veps[:, :], mv[:, :, 1], eps, None, ALU.add))
                link(nc.vector.tensor_scalar(half[:, :], veps[:, :].bitcast(i32), 1, None, ALU.logical_shift_right))
                link(nc.vector.tensor_scalar(rstd[:, :].bitcast(i32), half[:, :], -1.0, float(0x5f3759df),
                                             ALU.mult, ALU.add))
                for _ in range(NEWTON):
                    link(nc.vector.tensor_tensor(corr[:, :], rstd[:, :], rstd[:, :], ALU.mult))
                    link(nc.vector.scalar_tensor_tensor(corr[:, :], corr[:, :], -0.5, veps[:, :], ALU.mult, ALU.mult))
                    link(nc.vector.scalar_tensor_tensor(rstd[:, :], corr[:, :], 1.5, rstd[:, :], ALU.add, ALU.mult))

            def normalise(dst, src, it, b, done):
                for j in range(TB):
                    nc.vector.tensor_scalar(dst[:, j, :], src[:, tile_cols(it, TB * b + j)], mv[:, j, 0:1],
                                            rstd[:, j:j + 1], ALU.subtract, ALU.mult).then_inc(done, 1)

            def low_part(it, b, hi_there, count):
                dve.wait_ge(hi_there, count)
                cols = block_cols(it, b)
                return nc.vector.tensor_tensor(xl[:, cols], T_BANK[:, :], xh[:, cols], ALU.subtract).then_inc(t_read, 1)

            def over(t):
                return t[:, :].unsqueeze(2).to_broadcast([P, TB, NR])

            def pick(link, i, src):
                link(nc.vector.tensor_reduce(top[i][:, :], src, AX.X, ALU.max))
                link(nc.vector.tensor_tensor(rk[:, :, :], src, over(top[i]), ALU.is_equal))
                rv = rev[:, :].unsqueeze(1).to_broadcast([P, TB, NR])
                link(nc.vector.tensor_tensor(rk[:, :, :], rk[:, :, :], rv, ALU.mult))
                link(nc.vector.tensor_reduce(first[:, :], rk[:, :, :], AX.X, ALU.max))
                link(nc.vector.tensor_tensor(sel[i][:, :, :], rk[:, :, :], over(first), ALU.is_equal))

            def choose(f, it, b):
                link = chain(router_step, ROUTER_STEPS, f, it, b)
                dve.wait_ge(lg_psum, bcnt(1, f, it, b, 1))
                rbv = rb_sb[:, :].unsqueeze(1).to_broadcast([P, TB, NR])
                nc.vector.tensor_tensor(lg[:, :, :], T_BANK[:, 0:TB * NR].rearrange("p (t e) -> p t e", t=TB),
                                        rbv, ALU.add).then_inc(t_read, 1)
                dve.wait_ge(t_read, t_uses(f, it, b, "route") + 1)
                pick(link, 0, lg[:, :, :])
                link(nc.vector.scalar_tensor_tensor(lg2[:, :, :].rearrange("p t e -> p (t e)"),
                                                    sel[0][:, :, :].rearrange("p t e -> p (t e)"), NEG,
                                                    lg[:, :, :].rearrange("p t e -> p (t e)"), ALU.mult, ALU.add))
                pick(link, 1, lg2[:, :, :])
                link(nc.vector.tensor_tensor(diff[:, :], top[1][:, :], top[0][:, :], ALU.subtract))

            def weigh(f, it, b):
                link = chain(weight_step, WEIGHT_STEPS, f, it, b)
                dve.wait_ge(tanh_ready, bcnt(1, f, it, b, 1))
                nc.vector.tensor_scalar(wgt[0][:, :], tanh[:, :], -0.25 / W1_UP, 0.25 / W1_UP, ALU.mult, ALU.add)
                link(nc.vector.tensor_scalar(wgt[1][:, :], tanh[:, :], 0.25 / W1_UP, 0.25 / W1_UP, ALU.mult, ALU.add))
                nc.vector.tensor_tensor(sel[0][:, :, :], sel[0][:, :, :], over(wgt[0]), ALU.mult)
                link(nc.vector.tensor_tensor(sel[1][:, :, :], sel[1][:, :, :], over(wgt[1]), ALU.mult))
                nc.vector.tensor_tensor(comb[:, :, 0:NR], sel[0][:, :, :], sel[1][:, :, :], ALU.add).then_inc(comb_ready, 1)
                dve.wait_ge(comb_ready, bcnt(1, f, it, b, 1))

            def post_statistics(it, b):
                dve.wait_ge(acc_ready, bcnt(TB * NEX, 0, it, b, TB * NEX))
                statistics(chain(post_step, STAT_STEPS, 0, it, b), res2, it, b, EPS)

            def post_normalise(it, b):
                dve.wait_ge(xa_free, bcnt(1, 0, it, b, 1))
                normalise(xa, res2, it, b, post_xn)

            def ffn(f):
                def low(it, c):
                    e = c % NEX
                    for j in range(FC):
                        dve.wait_ge(hidh_ready, scnt(FC, f, it, c, j + 1))
                        nc.vector.tensor_tensor(hidl[e % HRING][:, j, :], h32[(FC * e + j) % len(h32)],
                                                hidh[e % HRING][:, j, :], ALU.subtract).then_inc(hidl_ready, 1)

                def combine(it, c):
                    e, b = c % NEX, c // NEX
                    dve.wait_ge(y_psum, scnt(TB, f, it, c, TB))
                    for j in range(TB):
                        if e > 0:
                            dve.wait_ge(acc_ready, scnt(TB, f, it, c, j + 1 - TB))
                        cols = tile_cols(it, TB * b + j)
                        nc.vector.scalar_tensor_tensor(res2[:, cols], Y_BANK[e % HRING][:, j * P:(j + 1) * P],
                                                       comb[:, j, e:e + 1], res2[:, cols],
                                                       ALU.mult, ALU.add).then_inc(acc_ready, 1)

                def step(it, c):
                    e, b = c % NEX, c // NEX
                    low(it, c)
                    if it is not None or c >= LAG:
                        combine(it, c - LAG)
                    if f == 0 and it is None:
                        for expert in SPLIT_AT.get(c, ()):
                            split_w1(expert)
                    if e == COMB_STEP:
                        weigh(f, it, b)
                    if f == 0 and (it is not None or b > 0):
                        if e == POST_STAT:
                            post_statistics(it, b - 1)
                        if e == POST_NORM:
                            post_normalise(it, b - 1)
                        if e == POST_T:
                            low_part(it, b - 1, post_xh, bcnt(1, 0, it, b - 1, 1))
                    if has_next(it, c):
                        if f == 1 and e == Y_STAT:
                            y_statistics(it, b + 1)
                        if f == 1 and e == Y_NORM:
                            y_normalise(it, b + 1)
                        if e == PRE_STEPS[f][0]:
                            pre_statistics(f, it, b + 1)
                        if e == PRE_STEPS[f][1]:
                            normalise(xn, res2, it, b + 1, pre_xn)
                        if e == PRE_T:
                            low_part(it, b + 1, pre_xh, bcnt(1, f, it, b + 1, 1))
                        if e == ROUTE:
                            choose(f, it, b + 1)
                run_steps(dve, f, step)
                for s in range(NEX * NBLK - LAG, NEX * NBLK):
                    combine(None, s)

            def y_statistics(it, b):
                statistics(chain(y_step, STAT_STEPS, 0, it, b), acc2, it, b, EPS_Y)

            def y_normalise(it, b):
                for j in range(TB):
                    nc.vector.scalar_tensor_tensor(xa[:, j, :], acc2[:, tile_cols(it, TB * b + j)], mv[:, j, 0:1],
                                                   gam[:, :], ALU.subtract, ALU.mult).then_inc(y_scaled, 1)
                for j in range(TB):
                    cols = tile_cols(it, TB * b + j)
                    dve.wait_ge(y_scaled, bcnt(TB, 0, it, b, j + 1))
                    nc.vector.scalar_tensor_tensor(res2[:, cols], xa[:, j, :], rstd[:, j:j + 1], res2[:, cols],
                                                   ALU.mult, ALU.add).then_inc(y_added, 1)

            def pre_statistics(f, it, b):
                if f == 0 and it is None:
                    dve.wait_ge(x_in[b], 16)
                elif f == 0:
                    for g in range(1, NBLK):
                        dve.wait_ge(x_in[g], 16)
                else:
                    dve.wait_ge(y_added, bcnt(TB, 0, it, b, TB))
                statistics(chain(pre_step, STAT_STEPS, f, it, b), res2, it, b, EPS)

            def split_w1(e):
                dve.wait_ge(w_hi, 2 * e + 1)
                cols = slice(e * F, (e + 1) * F)
                nc.vector.scalar_tensor_tensor(w1l[:, cols], stage[:, cols], W1_UP, w1h[:, cols],
                                               ALU.mult, ALU.subtract).then_inc(w1_ready, 1)

            def project_lo(it, c, g):
                r = (c + 3) % 2
                cols = slice(512 * g, 512 * g + 512)
                dve.wait_ge(hi_ready, cnt(2, it, c, 6 + g + 1))
                if g == 0:
                    wait_count(dve, stack_in, cnt(16 * 6, it, c, 2 * 16 * 6))
                nc.vector.scalar_tensor_tensor(ll[r][:, cols], J_BANK[:, :], 1.0 / WA_UP, hh[r][:, cols],
                                               ALU.mult, ALU.subtract).then_inc(lo_ready, 1)

            pre_statistics(0, None, 0)
            normalise(xn, res2, None, 0, pre_xn)
            split_w1(0)
            low_part(None, 0, pre_xh, 1)
            dve.wait_ge(const_ready, 1)
            dve.wait_ge(rw_in, 32)
            choose(0, None, 0)
            dve.wait_ge(w_hi, 2)
            nc.vector.scalar_tensor_tensor(w2l[:, 0, :], stage2[0], W1_UP, w2h[:, 0, :],
                                           ALU.mult, ALU.subtract).then_inc(w2_dve, 1)
            split_w1(1)
            ffn(0)
            post_statistics(None, NBLK - 1)
            project_lo(None, EARLY[0], 0)
            post_normalise(None, NBLK - 1)
            project_lo(None, EARLY[0], 1)
            low_part(None, NBLK - 1, post_xh, NBLK)
            for g in range(2):
                project_lo(None, EARLY[1], g)
            dve.wait_ge(const2_ready, 1)
            dve.wait_ge(xa_free, NBLK + 1)
            dve.wait_ge(beta_added, NBLK)

            def period(it, c):
                for k in range(NCH):
                    if live(c + 2, it, c):
                        i, k0, n = QCH[k]
                        dve.wait_ge(aux_done, cnt(NCH, it, c, 2 * NCH + k + 1))
                        if k == 0:
                            wait_count(dve, mhl_ready, cnt(3, it, c, 4))
                        nc.vector.tensor_reduce(mpart[:, i, k0 // 512:k0 // 512 + 1], A_BANK[k % 2][:, 0:n], AX.X,
                                                ALU.max).then_inc(max_done, 1)
                    if k - 1 in PROJ_SLOTS and projects(it, c):
                        project_lo(it, c, PROJ_SLOTS[k - 1])
                    k2, c2 = (k - 2) % NCH, c if k >= 2 else c - 1
                    if live(c2, it, c) and k2 not in POOL_LO:
                        n = KCH[k2][2]
                        dve.wait_ge(ph_ready, cnt(NCH, it, c2, k2 + 1))
                        nc.vector.tensor_tensor(pl[c2 % 2][:, POFF[k2]:POFF[k2] + n], p32[k2 % NRING][:, 0:n],
                                                ph[c2 % 2][:, POFF[k2]:POFF[k2] + n], ALU.subtract).then_inc(pl_ready, 1)
                    if k in (0, 1) and live(c + 1, it, c):
                        dve.wait_ge(mhl_ready, cnt(3, it, c, 4 + k))
                        if k == 0:
                            wait_count(dve, mT_psum, cnt(1, it, c, 1))
                            nc.vector.tensor_scalar(mhl[:, 0:QT], negm[:, :], 1.0 / M_UP, None,
                                                    ALU.mult).then_inc(mhl_ready, 1)
                        else:
                            nc.vector.scalar_tensor_tensor(mhl[:, QT:2 * QT], negm[:, :], 1.0 / M_UP, mhl[:, 0:QT],
                                                           ALU.mult, ALU.subtract).then_inc(mhl_ready, 1)
                    if k in (4, 11) and live(c - 1, it, c):
                        q = k // 11
                        dve.wait_ge(pv_done, cnt(2, it, c, -2 + q + 1))
                        o = O_BANK[q][:, 0:TB * VW].rearrange("p (i e) -> p i e", e=VW)
                        nc.vector.reciprocal(rsum[:, q, :], o[:, :, E]).then_inc(norm_done, 1)
                        dve.wait_ge(norm_done, cnt(4, it, c, -4 + 2 * q + 1))
                        half = slice(E * ((c - 1) // 2 % 2), E * ((c - 1) // 2 % 2) + E)
                        nc.vector.tensor_tensor(hpair[(c - 1) % 2][:, TB * q:TB * (q + 1), half], o[:, :, 0:E],
                                                rsum[:, q, :].unsqueeze(2).to_broadcast([P, TB, E]),
                                                ALU.mult).then_inc(norm_done, 1)
                    if k in WO_SLOTS and ends_pair(c - 2, it, c):
                        q = WO_SLOTS[k]
                        dve.wait_ge(wo_psum, pair_cnt(2, it, c - 2, q + 1))
                        wait_count(dve, y_ready, pair_cnt(2, it, c - 2, q))
                        t0 = QT * (c % 2) + TB * q
                        yv = acc[:, t0:t0 + TB, :].rearrange("p t d -> p (t d)")
                        nc.vector.tensor_tensor(yv, pair_banks(it, c, q)[1][:, :], yv, ALU.add).then_inc(y_ready, 1)
                if live(c + 2, it, c):
                    dve.wait_ge(max_done, cnt(NCH, it, c, 3 * NCH))
                    nc.vector.tensor_reduce(negm[:, :], mpart[:, :, :], AX.X, ALU.max, negate=True).then_inc(mhl_ready, 1)

            def first_block():
                dve.wait_ge(y_ready, NHEADS - 2)
                y_statistics(None, 0)
                y_normalise(None, 0)
                pre_statistics(1, None, 0)
                normalise(xn, res2, None, 0, pre_xn)
            run_periods(dve, period, before_last=first_block)
            dve.wait_ge(y_ready, NHEADS)
            low_part(None, 0, pre_xh, NBLK + 1)
            choose(1, None, 0)
            ffn(1)

        @block.tensor
        def _(pe):
            def transpose_block(src, done):
                for j in range(TB):
                    last = nc.tensor.transpose(T_BANK[0:src.shape[2], j * P:(j + 1) * P], src[:, j, :], identf[:, :])
                last.then_inc(done, 1)

            def transpose_pre(f, it, b):
                pe.wait_ge(pre_xn, bcnt(TB, f, it, b, TB))
                wait_count(pe, t_read, t_uses(f, it, b, "pre"))
                transpose_block(xn, pre_T)

            def transpose_post(it, b):
                pe.wait_ge(post_xn, bcnt(TB, 0, it, b, TB))
                pe.wait_ge(t_read, t_uses(0, it, b, "post"))
                transpose_block(xa, post_T)

            def router(f, it, b):
                pe.wait_ge(pre_xT, bcnt(1, f, it, b, 1))
                pe.wait_ge(t_read, t_uses(f, it, b, "route"))
                for j in range(TB):
                    last = nc.tensor.matmul(T_BANK[:, j * NR:(j + 1) * NR], xT[:, j * P:(j + 1) * P],
                                            rw_sb[:, :], start=True, stop=True)
                last.then_inc(lg_psum, 1)

            def ffn(f):
                def up(it, c, j):
                    e, b = c % NEX, c // NEX
                    if j == 0 and f == 0:
                        pe.wait_ge(w1_ready, e + 1)
                    wait_count(pe, h32_ready, scnt(FC, f, it, c, j + 1 - FC))
                    tok, w = block_cols(it, b), slice(e * F + j * P, e * F + (j + 1) * P)
                    with kept_addresses():
                        nc.tensor.matmul(H_BANK[j][:, :], w1h[:, w], xh[:, tok], start=True, stop=False)
                        nc.tensor.matmul(H_BANK[j][:, :], w1h[:, w], xl[:, tok], start=False, stop=False)
                        nc.tensor.matmul(H_BANK[j][:, :], w1l[:, w], xh[:, tok], start=False,
                                         stop=True).then_inc(h_psum, 1)

                def down(it, c, j):
                    e, b = c % NEX, c // NEX
                    if j == 0:
                        if f == 0:
                            pe.wait_ge(w2_pool if e else w2_dve, max(e, 1))
                            if e == NEX - 1:
                                pe.wait_ge(b2_scaled, 1)
                        if e == NEX - 1:
                            pe.wait_ge(t_read, t_uses(f, it, b, "comb") + 1)
                        wait_count(pe, acc_ready, scnt(TB, f, it, c, -TB * (HRING - 1)))
                        pe.wait_ge(hidl_ready, scnt(FC, f, it, c, FC))
                    y, tok, buf = Y_BANK[e % HRING][:, j * P:(j + 1) * P], slice(j * P, (j + 1) * P), e % HRING
                    if e == NEX - 1:
                        nc.tensor.matmul(y, combT[:, tok], b2[:, :], start=True, stop=False)
                    for k in range(FC):
                        wh, wl = w2h[:, e, k * D:(k + 1) * D], w2l[:, e, k * D:(k + 1) * D]
                        nc.tensor.matmul(y, hidh[buf][:, k, tok], wh, start=(k == 0 and e < NEX - 1), stop=False)
                        nc.tensor.matmul(y, hidh[buf][:, k, tok], wl, start=False, stop=False)
                        last = nc.tensor.matmul(y, hidl[buf][:, k, tok], wh, start=False, stop=(k == FC - 1))
                    last.then_inc(y_psum, 1)

                def step(it, c):
                    e, b = c % NEX, c // NEX
                    for work, n, j in ((up, 0, 0), (up, 0, 1), (down, LAG, 0), (down, LAG, 1),
                                       (up, 0, 2), (down, LAG, 2), (up, 0, 3), (down, LAG, 3)):
                        if it is not None or c - n >= 0:
                            work(it, c - n, j)
                        if (work, j) == (up, 3) and e == ROUTE and has_next(it, c):
                            router(f, it, b + 1)
                        if (work, j) != (up, 2):
                            continue
                        if e == CT_STEP:
                            pe.wait_ge(comb_ready, bcnt(1, f, it, b, 1))
                            pe.wait_ge(t_read, t_uses(f, it, b, "comb"))
                            transpose_block(comb, cT_psum)
                        if e == POST_T and f == 0 and (it is not None or b > 0):
                            transpose_post(it, b - 1)
                        if e == PRE_T and has_next(it, c):
                            transpose_pre(f, it, b + 1)

                transpose_pre(f, None, 0)
                router(f, None, 0)
                if f == 1:
                    pe.wait_ge(y_ready, NHEADS)
                run_steps(pe, f, step)
                for s in range(NEX * NBLK - LAG, NEX * NBLK):
                    for j in range(TB):
                        down(None, s, j)

            def project(it, c, g):
                wait_count(pe, lo_ready, cnt(2, it, c, 6 + g))
                if g == 0:
                    wait_count(pe, mrows_ready, cnt(1, it, c, 1))
                wcol = bass.ds(head_of(it, c + 3) * P, P)
                t0 = ((c + 3) % 2) * S + 512 * g
                with kept_addresses():
                    nc.tensor.matmul(J_BANK[:, :], wqk_h[:, wcol], xh[:, t0:t0 + 512], start=True, stop=False)
                    nc.tensor.matmul(J_BANK[:, :], wqk_h[:, wcol], xl[:, t0:t0 + 512], start=False, stop=False)
                    nc.tensor.matmul(J_BANK[:, :], wqk_l[:, wcol], xh[:, t0:t0 + 512], start=False,
                                     stop=True).then_inc(proj_done, 1)

            pe.wait_ge(const_ready, 1)
            pe.wait_ge(rw_in, 32)
            ffn(0)
            pe.wait_ge(acc_ready, TB * NEX * NBLK)
            pe.wait_ge(wa_ready, 3)
            for g in range(2):
                project(None, EARLY[0], g)
            transpose_post(None, NBLK - 1)
            pe.wait_ge(t_read, 4 * NBLK)
            for g in range(2):
                project(None, EARLY[1], g)
            pe.wait_ge(const2_ready, 1)
            pe.wait_ge(wo_in, 48)

            def period(it, c):
                m = c - 1
                waited = set()
                for k in range(NCH):
                    if live(c, it, c):
                        j, q0, n = KCH[k]
                        b = c % 4
                        if k == 0:
                            pe.wait_ge(stack_in, cnt(16 * 6, it, c, 16 * 6))
                            pe.wait_ge(mrow_in, cnt(16, it, c, 16))
                        wait_count(pe, exp_done, cnt(NCH, it, c, k - 1))
                        dst, keys = S_BANK[k % 2][:, 0:n], slice(j * P, (j + 1) * P)
                        nc.tensor.matmul(dst, ks[b][:, keys], qs[b][:, q0:q0 + n], start=True, stop=False)
                        nc.tensor.matmul(dst, km[b][:, keys], qm[b][:, q0:q0 + n], start=False,
                                         stop=True).then_inc(main_done, 1)
                    if live(c + 2, it, c):
                        i, k0, n = QCH[k]
                        b = (c + 2) % 4
                        if k == 0:
                            pe.wait_ge(stack_in, cnt(16 * 6, it, c, 3 * 16 * 6))
                        wait_count(pe, max_done, cnt(NCH, it, c, 2 * NCH + k - 1))
                        diag = k0 + n == P * (i + 1)
                        last = nc.tensor.matmul(A_BANK[k % 2][:, 0:n], qs[b][:, i * P:(i + 1) * P], ks[b][:, k0:k0 + n],
                                                start=True, stop=not diag)
                        if diag:
                            last = nc.tensor.matmul(A_BANK[k % 2][:, n - P:n], identb[:, :], tri[:, :],
                                                    start=False, stop=True)
                        last.then_inc(aux_done, 1)
                    if k == MT_SLOT and live(c + 1, it, c):
                        v = cnt(2, it, c, 8)
                        pe.wait_ge(lo_ready, min(v, 2 * NHEADS) if it is None else v)
                        pe.wait_ge(mhl_ready, cnt(3, it, c, 6))
                        nc.tensor.transpose(J_BANK[:, :].bitcast(f16)[0:2 * QT, 0:P], mhl[:, :],
                                            identh[:, :]).then_inc(mT_psum, 1)
                    if k in PROJ_SLOTS and projects(it, c):
                        project(it, c, PROJ_SLOTS[k])
                    if k in T_SLOTS and ends_pair(c - 2, it, c):
                        q = T_SLOTS[k]
                        bank_t, shared = pair_banks(it, c, q)[0], pair_banks(it, c, q)[0] is V_BANK
                        if q == 0:
                            pe.wait_ge(norm_done, cnt(4, it, c, -4))
                            v = cnt(1, it, c, 1)
                            pe.wait_ge(v32_ready, min(v, NHEADS) if it is None else v)
                        elif shared:
                            pe.wait_ge(hT_ready, pair_cnt(2, it, c - 2, 1))
                        for j in range(TB):
                            last = nc.tensor.transpose(bank_t[:, j * P:(j + 1) * P], hpair[c % 2][:, TB * q + j, :],
                                                       identf[:, :])
                        last.then_inc(hT_psum, 1)
                    if k in WO_SLOTS and ends_pair(c - 2, it, c):
                        q = WO_SLOTS[k]
                        bank_y, shared = pair_banks(it, c, q)[1], pair_banks(it, c, q)[1] is V_BANK
                        pe.wait_ge(hT_ready, pair_cnt(2, it, c - 2, 2))
                        if q == 1 and shared:
                            pe.wait_ge(y_ready, pair_cnt(2, it, c - 2, 1))
                        pair = (c - 2) // 4 if it is None else it + (c - 2) // 4
                        with kept_addresses():
                            for j in range(TB):
                                last = nc.tensor.matmul(bank_y[:, j * P:(j + 1) * P], hpT[q][:, j * P:(j + 1) * P],
                                                        wo_sb[:, bass.ds(pair, 1), :], start=True, stop=True)
                        last.then_inc(wo_psum, 1)
                    if k == V_SLOT and live(c + 1, it, c):
                        if ends_pair(c - 2, it, c):
                            pe.wait_ge(y_ready, pair_cnt(2, it, c - 2, 2))
                        wait_count(pe, v32_ready, cnt(1, it, c, 1))
                        wv = bass.ds(head_of(it, c + 1) * E, E)
                        with kept_addresses():
                            for j in range(QT):
                                tok = slice(((c + 1) % 2) * S + j * P, ((c + 1) % 2) * S + (j + 1) * P)
                                dst = V_BANK[:, j * E:(j + 1) * E]
                                nc.tensor.matmul(dst, xh[:, tok], wv_h[:, wv], start=True, stop=False)
                                nc.tensor.matmul(dst, xh[:, tok], wv_l[:, wv], start=False, stop=False)
                                last = nc.tensor.matmul(dst, xl[:, tok], wv_h[:, wv], start=False, stop=True)
                        last.then_inc(v_psum, 1)
                    if live(m, it, c):
                        for i, j in BLOCKS[BPS * k:BPS * (k + 1)]:
                            q = i // TB
                            if (i, j) == (0, 0):
                                pe.wait_ge(vl_ready, cnt(1, it, c, 0))
                            if j == 0 and i % TB == 0:
                                wait_count(pe, norm_done, cnt(4, it, c, -8 + 2 * q + 2))
                            ch = KIDX[(j, q)]
                            if ch not in waited:
                                wait_split(pe, it, m, ch)
                            waited.add(ch)
                            cols = slice(POFF[ch] + i * P - KCH[ch][1], POFF[ch] + i * P - KCH[ch][1] + P)
                            o = O_BANK[q][:, (i % TB) * VW:(i % TB + 1) * VW]
                            nc.tensor.matmul(o, ph[m % 2][:, cols], vh[m % 4][:, j, :], start=(j == 0), stop=False)
                            nc.tensor.matmul(o[:, 0:E], ph[m % 2][:, cols], vl[m % 4][:, j, :], start=False, stop=False)
                            last = nc.tensor.matmul(o, pl[m % 2][:, cols], vh[m % 4][:, j, :], start=False, stop=(j == i))
                            if i == j and i % TB == TB - 1:
                                last.then_inc(pv_done, 1)
            run_periods(pe, period)
            ffn(1)


def kernel(L0_attn_x, L0_attn_Wq, L0_attn_Wk, L0_attn_Wv, L0_attn_Wo, L0_attn_gamma, L0_attn_beta,
           L0_ffn_shared_w1, L0_ffn_shared_b1, L0_ffn_shared_w2, L0_ffn_shared_b2, L0_ffn_router_w, L0_ffn_router_b,
           L0_ffn_spec_w1, L0_ffn_spec_b1, L0_ffn_spec_w2, L0_ffn_spec_b2):
    import numpy as np
    import concourse.bacc as bacc
    from concourse.bass_utils import run_bass_kernel_spmd

    P = 128
    B, S, D = L0_attn_x.shape
    NEX, F, _ = L0_ffn_spec_w1.shape
    NT, FC = B * S // P, F // P
    laid = {
        "x": L0_attn_x.reshape(NT, P, D).transpose(1, 0, 2),
        "w1s": L0_ffn_shared_w1.T,
        "w1e": L0_ffn_spec_w1.transpose(2, 0, 1),
        "w2s": L0_ffn_shared_w2.T.reshape(FC, P, D).transpose(1, 0, 2),
        "w2e": L0_ffn_spec_w2.transpose(2, 0, 1).reshape(FC, P, NEX, D).transpose(1, 2, 0, 3),
        "b1s": L0_ffn_shared_b1.reshape(FC, P).T,
        "b1e": L0_ffn_spec_b1.reshape(NEX, FC, P).transpose(2, 0, 1),
        "b2s": L0_ffn_shared_b2.reshape(1, D),
        "b2e": L0_ffn_spec_b2,
        "rw": L0_ffn_router_w.T,
        "rb": L0_ffn_router_b,
        "wq": L0_attn_Wq.transpose(1, 0, 2),
        "wk": L0_attn_Wk.transpose(1, 0, 2),
        "wv": L0_attn_Wv.transpose(1, 0, 2),
        "wo": L0_attn_Wo.reshape(-1, P, D).transpose(1, 0, 2),
        "gamma": L0_attn_gamma,
        "beta": L0_attn_beta,
    }
    nc = bacc.Bacc("TRN2", target_bir_lowering=False, num_devices=1)
    arrays = {n: np.ascontiguousarray(a) for n, a in laid.items()}
    args = [nc.dram_tensor(n, a.shape, mybir.dt.from_np(a.dtype), kind="ExternalInput").ap() for n, a in arrays.items()]
    out = nc.dram_tensor("out", (P, NT, D), mybir.dt.float32, kind="ExternalOutput").ap()
    macaron_block_kernel(nc, *args, out)
    r = run_bass_kernel_spmd(nc, [arrays], core_ids=[0])
    y = r.results[0]["out"]
    return y.transpose(1, 0, 2).reshape(B, S, D)
```
